# Optimizing a Trainium2 kernel written in Bass

```python
import numpy as np
import jax
import jax.numpy as jnp

def _softmax(x, axis=-1):
    return jax.nn.softmax(x, axis=axis)

def _gelu(x):
    return jax.nn.gelu(x, approximate=True)

def _silu(x):
    return jax.nn.silu(x)

def _sigmoid(x):
    return jax.nn.sigmoid(x)

def _layernorm(x, axis=-1, eps=1e-05):
    m = jnp.mean(x, axis=axis, keepdims=True)
    v = jnp.var(x, axis=axis, keepdims=True)
    return (x - m) / jnp.sqrt(v + eps)

def _scatter_add(tgt, idx, src, axis=0):
    return tgt.at[idx].add(src)

def _segment_sum(src, seg, n):
    return jax.ops.segment_sum(src, seg, n)
kernel_name = 'mk_audio_tower_d1_tok_audfeat1024_r4_b59509'

def setup_inputs(seed: int=0):
    np.random.seed(seed)
    _w = jnp.asarray

    def _rec_inputs():
        import jax
        import jax.numpy as jnp
        _rk = jax.random.key(seed)
        x = -0.000494162 + 1.00033 * jax.random.normal(jax.random.fold_in(_rk, 1), (64, 1, 750), jnp.float32)
        return x
    x = _rec_inputs()

    def _L0_tok_setup():
        import jax, jax.numpy as jnp
        import numpy as np
        from jax import lax
        B, C_IN, L = (8, 1, 120000)
        DIMS, HEAD = (256, 16)
        HEAD_DIM = DIMS // HEAD
        GROUPS = DIMS // 8

        def _conv1d(x, w, b, stride, pad, groups=1):
            y = lax.conv_general_dilated(x, w, window_strides=(stride,), padding=[(pad, pad)], dimension_numbers=('NCH', 'OIH', 'NCH'), feature_group_count=groups)
            return y + b[None, :, None]

        def _gelu(v):
            return jax.nn.gelu(v, approximate=False)
        key = jax.random.key(seed)
        ks = jax.random.split(key, 12)
        s = 0.02
        inp = {'x': jax.random.normal(ks[0], (B, C_IN, L), dtype=jnp.float32), 'w1': jax.random.normal(ks[1], (DIMS // 8, C_IN, 15), dtype=jnp.float32) * s, 'b1': jnp.zeros((DIMS // 8,), dtype=jnp.float32), 'w2': jax.random.normal(ks[2], (DIMS // 4, DIMS // 8, 7), dtype=jnp.float32) * s, 'b2': jnp.zeros((DIMS // 4,), dtype=jnp.float32), 'w3': jax.random.normal(ks[3], (DIMS, DIMS // 4, 9), dtype=jnp.float32) * s, 'b3': jnp.zeros((DIMS,), dtype=jnp.float32), 'w4': jax.random.normal(ks[4], (DIMS, DIMS // GROUPS, 3), dtype=jnp.float32) * s, 'b4': jnp.zeros((DIMS,), dtype=jnp.float32), 'w5': jax.random.normal(ks[5], (DIMS, DIMS, 1), dtype=jnp.float32) * s, 'b5': jnp.zeros((DIMS,), dtype=jnp.float32), 'rope_freqs': 1.0 / 50.0 ** (jnp.arange(0, HEAD_DIM, 2, dtype=jnp.float32) / HEAD_DIM), 'norm_w': jnp.ones((DIMS,), dtype=jnp.float32)}
        return inp
    _L0_tok_all = _L0_tok_setup()
    _L0_tok_in = {k: v for k, v in _L0_tok_all.items() if k in ('w1', 'b1', 'w2', 'b2', 'w3', 'b3', 'w4', 'b4', 'w5', 'b5', 'rope_freqs', 'norm_w')}
    del _L0_tok_all

    def _L0_attn_setup():
        import jax, jax.numpy as jnp
        import numpy as np
        HEADS = 32
        DIM_HEAD = 32
        EPS = 1e-06
        key = jax.random.key(seed)
        k1, k2, k3 = jax.random.split(key, 3)
        b, n, dim = (2, 512, 256)
        x = jax.random.normal(k1, (b, n, dim), dtype=jnp.float32)
        w_qkv = jax.random.normal(k2, (dim, 3 * HEADS * DIM_HEAD), dtype=jnp.float32) * dim ** (-0.5)
        w_out = jax.random.normal(k3, (HEADS * DIM_HEAD, dim), dtype=jnp.float32) * dim ** (-0.5)
        b_out = jnp.zeros((dim,), dtype=jnp.float32)
        ln_gamma = jnp.ones((dim,), dtype=jnp.float32)
        ln_beta = jnp.zeros((dim,), dtype=jnp.float32)
        return {'x': x, 'w_qkv': w_qkv, 'w_out': w_out, 'b_out': b_out, 'ln_gamma': ln_gamma, 'ln_beta': ln_beta}
    _L0_attn_all = _L0_attn_setup()
    _L0_attn_in = {k: v for k, v in _L0_attn_all.items() if k in ('w_qkv', 'w_out', 'b_out', 'ln_gamma', 'ln_beta')}
    del _L0_attn_all

    def _L0_ffn_setup():
        import jax, jax.numpy as jnp
        import numpy as np
        TOP_K = 2
        key = jax.random.key(seed)
        kx, kg, k1, k2 = jax.random.split(key, 4)
        B, T, D, E, H = (4, 256, 256, 8, 512)
        x = jax.random.normal(kx, (B, T, D), dtype=jnp.float32)
        Wg = jax.random.normal(kg, (D, E), dtype=jnp.float32) * 0.02
        W1 = jax.random.normal(k1, (E, D, H), dtype=jnp.float32) * 0.02
        W2 = jax.random.normal(k2, (E, H, D), dtype=jnp.float32) * 0.02
        return {'x': x, 'Wg': Wg, 'W1': W1, 'W2': W2}
    _L0_ffn_all = _L0_ffn_setup()
    _L0_ffn_in = {k: v for k, v in _L0_ffn_all.items() if k in ('Wg', 'W1', 'W2')}
    del _L0_ffn_all
    return {'x': x, 'L0_tok_w1': _L0_tok_in['w1'], 'L0_tok_b1': _L0_tok_in['b1'], 'L0_tok_w2': _L0_tok_in['w2'], 'L0_tok_b2': _L0_tok_in['b2'], 'L0_tok_w3': _L0_tok_in['w3'], 'L0_tok_b3': _L0_tok_in['b3'], 'L0_tok_w4': _L0_tok_in['w4'], 'L0_tok_b4': _L0_tok_in['b4'], 'L0_tok_w5': _L0_tok_in['w5'], 'L0_tok_b5': _L0_tok_in['b5'], 'L0_tok_rope_freqs': _L0_tok_in['rope_freqs'], 'L0_tok_norm_w': _L0_tok_in['norm_w'], 'L0_attn_w_qkv': _L0_attn_in['w_qkv'], 'L0_attn_w_out': _L0_attn_in['w_out'], 'L0_attn_b_out': _L0_attn_in['b_out'], 'L0_attn_ln_gamma': _L0_attn_in['ln_gamma'], 'L0_attn_ln_beta': _L0_attn_in['ln_beta'], 'L0_ffn_Wg': _L0_ffn_in['Wg'], 'L0_ffn_W1': _L0_ffn_in['W1'], 'L0_ffn_W2': _L0_ffn_in['W2']}

def reference(x, L0_tok_w1, L0_tok_b1, L0_tok_w2, L0_tok_b2, L0_tok_w3, L0_tok_b3, L0_tok_w4, L0_tok_b4, L0_tok_w5, L0_tok_b5, L0_tok_rope_freqs, L0_tok_norm_w, L0_attn_w_qkv, L0_attn_w_out, L0_attn_b_out, L0_attn_ln_gamma, L0_attn_ln_beta, L0_ffn_Wg, L0_ffn_W1, L0_ffn_W2):
    import jax
    import jax.numpy as jnp

    def _L0_tok_ref(x, w1, b1, w2, b2, w3, b3, w4, b4, w5, b5, rope_freqs, norm_w):
        import jax, jax.numpy as jnp
        import numpy as np
        from jax import lax
        B, C_IN, L = (8, 1, 120000)
        DIMS, HEAD = (256, 16)
        HEAD_DIM = DIMS // HEAD
        GROUPS = DIMS // 8

        def _conv1d(x, w, b, stride, pad, groups=1):
            y = lax.conv_general_dilated(x, w, window_strides=(stride,), padding=[(pad, pad)], dimension_numbers=('NCH', 'OIH', 'NCH'), feature_group_count=groups)
            return y + b[None, :, None]

        def _gelu(v):
            return jax.nn.gelu(v, approximate=False)
        h = _gelu(_conv1d(x, w1, b1, stride=8, pad=7))
        h = _gelu(_conv1d(h, w2, b2, stride=4, pad=3))
        h = _gelu(_conv1d(h, w3, b3, stride=5, pad=4))
        h = _gelu(_conv1d(h, w4, b4, stride=1, pad=1, groups=GROUPS))
        h = _gelu(_conv1d(h, w5, b5, stride=1, pad=0))
        h = jnp.transpose(h, (0, 2, 1))
        Bb, T, D = h.shape
        xh = h.reshape(Bb, T, HEAD, HEAD_DIM).transpose(0, 2, 1, 3)
        t = jnp.arange(T, dtype=jnp.float32)
        ang = t[:, None] * rope_freqs[None, :]
        cos, sin = (jnp.cos(ang), jnp.sin(ang))
        xp = xh.reshape(Bb, HEAD, T, HEAD_DIM // 2, 2)
        xr, xi = (xp[..., 0], xp[..., 1])
        out_r = xr * cos - xi * sin
        out_i = xr * sin + xi * cos
        xh = jnp.stack([out_r, out_i], axis=-1).reshape(Bb, HEAD, T, HEAD_DIM)
        h = xh.transpose(0, 2, 1, 3).reshape(Bb, T, D)
        ms = jnp.mean(h * h, axis=-1, keepdims=True)
        return h * jax.lax.rsqrt(ms + 1e-08) * norm_w

    def _L0_attn_ref(x, w_qkv, w_out, b_out, ln_gamma, ln_beta):
        import jax, jax.numpy as jnp
        import numpy as np
        HEADS = 32
        DIM_HEAD = 32
        EPS = 1e-06
        b, n, dim = x.shape
        scale = DIM_HEAD ** (-0.5)
        qkv = x @ w_qkv
        qkv = qkv.reshape(b, n, 3, HEADS, DIM_HEAD)
        qkv = jnp.transpose(qkv, (2, 0, 3, 1, 4))
        q, k, v = (qkv[0], qkv[1], qkv[2])
        dots = jnp.einsum('bhnd,bhmd->bhnm', q, k) * scale
        attn = jax.nn.softmax(dots, axis=-1)
        out = jnp.einsum('bhnm,bhmd->bhnd', attn, v)
        out = jnp.transpose(out, (0, 2, 1, 3)).reshape(b, n, HEADS * DIM_HEAD)
        out = out @ w_out + b_out
        mu = jnp.mean(out, axis=-1, keepdims=True)
        var = jnp.mean((out - mu) ** 2, axis=-1, keepdims=True)
        out = (out - mu) / jnp.sqrt(var + EPS) * ln_gamma + ln_beta
        return out

    def _L0_ffn_ref(x, Wg, W1, W2):
        import jax, jax.numpy as jnp
        import numpy as np
        TOP_K = 2
        B, T, D = x.shape
        E = W1.shape[0]
        logits = jnp.einsum('btd,de->bte', x, Wg)
        probs = jax.nn.softmax(logits, axis=-1)
        top_w, top_i = jax.lax.top_k(probs, TOP_K)
        top_w = top_w / (jnp.sum(top_w, axis=-1, keepdims=True) + 1e-08)
        N = B * T
        oh = jax.nn.one_hot(top_i.reshape(N, TOP_K), E, dtype=x.dtype)
        combine = jnp.sum(oh * top_w.reshape(N, TOP_K)[..., None], axis=1)
        xt = x.reshape(N, D)
        h = jnp.einsum('td,edh->teh', xt, W1)
        h = jnp.square(jax.nn.relu(h))
        y = jnp.einsum('teh,ehd->ted', h, W2)
        out = jnp.einsum('te,ted->td', combine, y)
        return out.reshape(B, T, D)
    h = _L0_tok_ref(x, L0_tok_w1, L0_tok_b1, L0_tok_w2, L0_tok_b2, L0_tok_w3, L0_tok_b3, L0_tok_w4, L0_tok_b4, L0_tok_w5, L0_tok_b5, L0_tok_rope_freqs, L0_tok_norm_w)
    h = h + _L0_attn_ref(_layernorm(h, axis=-1), L0_attn_w_qkv, L0_attn_w_out, L0_attn_b_out, L0_attn_ln_gamma, L0_attn_ln_beta)
    h = h + _L0_ffn_ref(_layernorm(h, axis=-1), L0_ffn_Wg, L0_ffn_W1, L0_ffn_W2)
    return h

_drawn_inputs = setup_inputs


def setup_inputs(seed=0):
    import zlib

    import numpy as np

    out = dict(_drawn_inputs(seed))
    spreads = {'L0_tok_b1': (0.0, 0.8),
     'L0_tok_b2': (0.0, 0.8),
     'L0_tok_b3': (0.0, 0.8),
     'L0_tok_b4': (0.0, 0.535),
     'L0_tok_b5': (0.0, 0.1),
     'L0_tok_norm_w': (1.0, 0.2),
     'L0_attn_b_out': (0.0, 0.1),
     'L0_attn_ln_gamma': (1.0, 0.2),
     'L0_attn_ln_beta': (0.0, 0.1)}
    factors = {'x': 8.0,
     'L0_tok_w1': 8.0,
     'L0_tok_w2': 8.0,
     'L0_tok_w3': 8.0,
     'L0_tok_w4': 6.597,
     'L0_ffn_Wg': 2.984}
    for name, (base, spread) in spreads.items():
        noise = np.random.default_rng([zlib.crc32(name.encode()), seed]).standard_normal(out[name].shape)
        drawn = base * np.exp(spread * noise) if base else spread * noise
        out[name] = jnp.asarray(drawn.astype(out[name].dtype))
    for name, factor in factors.items():
        out[name] = (out[name] * factor).astype(out[name].dtype)
    return out
```

```python
from contextlib import ExitStack

import concourse.bass as bass
from concourse import mybir

F32 = mybir.dt.float32
F32R = mybir.dt.float32r
BF16 = mybir.dt.bfloat16
ALU = mybir.AluOpType
ACT = mybir.ActivationFunctionType
AX = mybir.AxisListType

P = 128
CLIPS = 64
FRAMES = 5
DIM = 256
KC = DIM // P
HEADS, HEAD_DIM = 32, 32
INNER = HEADS * HEAD_DIM
HC = INNER // P
EXPERTS, HIDDEN = 8, 512
HK = HIDDEN // P
Q4 = 4

GROUP_CLIPS = 6
GT = GROUP_CLIPS * FRAMES
GROUPS = -(-CLIPS // GROUP_CLIPS)
STACKS = -(-GROUPS // Q4)
SLOTS = STACKS * P
TOK = GROUPS * GT
FULL_GROUPS = CLIPS // GROUP_CLIPS
REST_CLIPS = CLIPS - FULL_GROUPS * GROUP_CLIPS

C1, K1, S1, PAD1 = 32, 15, 8, 7
PER = 4
WINDOW = S1 * (PER - 1) + K1
L1 = 94
BLOCKS = 24
C2, K2, PAD2 = 64, 7, 3
L2 = 24
C3, K3, S3, PAD3 = 256, 9, 5, 4
PAIRS = (K3 + 1) // 2
H2_COLS = PAD3 + L2 + 1
BANK = 512
C1_STEP = BANK // CLIPS
C_PARTS = BLOCKS // C1_STEP

ROUNDS = HC // 2
COMBOS = 2 * STACKS
SCOLS = COMBOS * GT
PROJ_BANK = 4
RAW_SLOTS, SPLIT_SLOTS = 4, 3
ECOLS = KC * HIDDEN + HK * DIM

SCALE = float(HEAD_DIM) ** -0.5
PI = 3.14159265358979
TWO_PI_HI, TWO_PI_MID, TWO_PI_LO = 6.28125, 1.9353071693331003e-03, 1.025271e-11
ROUNDER = 12582912.0
LN_EPS, RMS_EPS, ATT_EPS, TOP_EPS = 1e-5, 1e-8, 1e-6, 1e-8

COL_B1, COL_B2, COL_B3, COL_B4 = 0, 1, 2, 4
ROW_NORM, ROW_BOUT, ROW_GAMMA, ROW_BETA = range(4)


def build(nc, xw, w1, w2, w3, w4, w5, bias_cols, b5, rows, freqs, w_qkv, w_out, w_gate, W1, W2,
          tcol, phase, sign, ident, mask_q, mask_k, out):
    with ExitStack() as ctx:
        def sb(name, shape, dt=F32, life=ctx):
            return life.enter_context(nc.sbuf_tensor(name, shape, dt))

        def sem(name):
            return ctx.enter_context(nc.semaphore(name))

        with ExitStack() as conv:
            xw_s = sb("xw_s", [WINDOW, BLOCKS * CLIPS], life=conv)
            w1_s = sb("w1_s", [WINDOW, P], life=conv)
            w2_s = sb("w2_s", [P, 2, C2], life=conv)
            w3_s = sb("w3_s", [P, PAIRS, C3], life=conv)
            w4_s = sb("w4_s", [P, KC, 3, P], life=conv)
            w5_s = sb("w5_s", [P, KC, DIM], life=conv)
            h1 = sb("h1", [P, (BLOCKS + 1) * CLIPS], life=conv)
            h2 = sb("h2", [P, H2_COLS, CLIPS], life=conv)
            h3 = sb("h3", [P, KC, FRAMES + 2, CLIPS], life=conv)
            h4 = sb("h4", [P, KC, SLOTS], life=conv)
        raw = sb("raw", [P, RAW_SLOTS, ECOLS])
        sb("conv_rest", [P, 1280])
        with ExitStack() as early:
            qkv_raw = sb("qkv_raw", [P, KC, 3 * INNER], life=early)
        att_hi = sb("att_hi", [P, HC, SLOTS], F32R)
        att_lo = sb("att_lo", [P, HC, SLOTS], F32R)
        with ExitStack() as early:
            qkv_hi = sb("qkv_hi", [P, KC, 3 * INNER], F32R, life=early)
            qkv_lo = sb("qkv_lo", [P, KC, 3 * INNER], F32R, life=early)
        exp_hi = sb("exp_hi", [P, SPLIT_SLOTS, ECOLS], F32R)
        exp_lo = sb("exp_lo", [P, SPLIT_SLOTS, ECOLS], F32R)

        with ExitStack() as early:
            qT = sb("qT", [P, HC, TOK], life=early)
            kT = sb("kT", [P, HC, TOK], life=early)
            v_s = sb("v_s", [P, STACKS, INNER], life=early)
        hid_hi = sb("hid_hi", [P, 2 * HK, SLOTS], F32R)
        hid_lo = sb("hid_lo", [P, 2 * HK, SLOTS], F32R)
        relu = sb("relu", [P, 2, TOK])
        sq = sb("sq", [P, 2, TOK])
        sb("early_rest", [P, 1000])

        wout_hi = sb("wout_hi", [P, HC, DIM], F32R)
        wout_lo = sb("wout_lo", [P, HC, DIM], F32R)
        cols_s = sb("cols_s", [P, 6])
        b5_s = sb("b5_s", [1, DIM])
        ones_s = sb("ones_s", [1, P])
        rows_s = sb("rows_s", [P, 4, DIM])
        freq_s = sb("freq_s", [P, 32])
        tcol_s = sb("tcol_s", [P, 1])
        phase_s = sb("phase_s", [P, 32])
        sign_s = sb("sign_s", [P, 32])
        ident_s = sb("ident_s", [P, P])
        maskq_f = sb("maskq_f", [P, P])
        maskk_f = sb("maskk_f", [P, SCOLS])
        maskq_s = sb("maskq_s", [P, P], BF16)
        maskk_s = sb("maskk_s", [P, SCOLS], BF16)
        gate_s = sb("gate_s", [P, KC, EXPERTS])
        ang = sb("ang", [P, 6, 32])
        table = sb("table", [P, 32])
        x5 = sb("x5", [P, STACKS, DIM])
        ropa = sb("ropa", [P, STACKS, DIM])
        ropb = sb("ropb", [P, STACKS, DIM])
        h = sb("h", [P, STACKS, DIM])
        xn = sb("xn", [P, STACKS, DIM])
        power = sb("power", [P, STACKS])
        ssq = sb("ssq", [P, STACKS])
        var = sb("var", [P, STACKS])
        rstd = sb("rstd", [P, 4, STACKS])
        stats = sb("stats", [P, STACKS, 6])
        mv = sb("mv", [P, 3, STACKS, 2])
        xT_hi = sb("xT_hi", [P, KC, SLOTS], F32R)
        xT_lo = sb("xT_lo", [P, KC, SLOTS], F32R)
        xT_f = ropa[:].rearrange("p s d -> p (s d)").rearrange("p (k n) -> p k n", k=KC)
        prob = sb("prob", [P, Q4 * COMBOS, 32])
        probT = sb("probT", [P, 2, Q4 * COMBOS, 32])
        smax = sb("smax", [P, Q4 * COMBOS])
        ssum = sb("ssum", [P, Q4 * COMBOS])
        logit = sb("logit", [P, STACKS, EXPERTS])
        gmax = sb("gmax", [P, STACKS])
        gsum = sb("gsum", [P, STACKS])
        gprob = sb("gprob", [P, STACKS, 16])
        gtop = sb("gtop", [P, STACKS, 8])
        gfind = sb("gfind", [P, STACKS, 8])
        gleft = sb("gleft", [P, STACKS, 16])
        comb = sb("comb", [P, STACKS, EXPERTS])

        ps = ctx.enter_context(nc.psum_tensor("ps", [P, 8, BANK], F32))

        ld_x = sem("ld_x")
        ld_w2 = sem("ld_w2")
        ld_w3 = sem("ld_w3")
        ld_w45 = sem("ld_w45")
        ld_rope = sem("ld_rope")
        ld_rows = sem("ld_rows")
        ld_misc = sem("ld_misc")
        ld_qkv = [sem(f"ld_qkv{i}") for i in range(6)]
        ld_raw = [sem(f"ld_raw{i}") for i in range(RAW_SLOTS)]
        pad_zero, end_zero = sem("pad_zero"), sem("end_zero")
        const_ready = sem("const_ready")
        conv1_mm, conv1_act = sem("conv1_mm"), sem("conv1_act")
        conv2_mm, conv2_act, conv2_up = sem("conv2_mm"), sem("conv2_act"), sem("conv2_up")
        conv3_mm, conv3_act = sem("conv3_mm"), sem("conv3_act")
        conv4_mm, conv4_act = sem("conv4_mm"), sem("conv4_act")
        conv5_mm, conv5_act = sem("conv5_mm"), sem("conv5_act")
        angle, sines, table_ready = sem("angle"), sem("sines"), sem("table_ready")
        rope_a, rope_b, rope_y = sem("rope_a"), sem("rope_b"), sem("rope_y")
        squares, rstd_var, rstd_ready = sem("squares"), sem("rstd_var"), sem("rstd_ready")
        h_ready, stat_ready, mv_ready = sem("h_ready"), sem("stat_ready"), sem("mv_ready")
        xn_ready, xT_mm, xT_high, xT_low = sem("xn_ready"), sem("xT_mm"), sem("xT_high"), sem("xT_low")
        xT_full = sem("xT_full")
        qkv_high, qkv_low = sem("qkv_high"), sem("qkv_low")
        proj_mm, proj_out = sem("proj_mm"), sem("proj_out")
        score_mm, s_max, s_shift, s_exp = sem("score_mm"), sem("s_max"), sem("s_shift"), sem("s_exp")
        s_sum, s_inv, s_norm, s_turn = sem("s_sum"), sem("s_inv"), sem("s_norm"), sem("s_turn")
        pv_mm, att_high, att_low, att_zero = sem("pv_mm"), sem("att_high"), sem("att_low"), sem("att_zero")
        out_mm, out_bias = sem("out_mm"), sem("out_bias")
        ln_z, ln_zg, hb_ready = sem("ln_z"), sem("ln_zg"), sem("hb_ready")
        raw_high, raw_low = sem("raw_high"), sem("raw_low")
        gate_mm, g_step, g_exp, comb_ready = sem("gate_mm"), sem("g_step"), sem("g_exp"), sem("comb_ready")
        up_mm, relu_done, sq_done = sem("up_mm"), sem("relu_done"), sem("sq_done")
        hid_high, hid_low = sem("hid_high"), sem("hid_low")
        down_mm, mixed = sem("down_mm"), sem("mixed")
        stored = sem("stored")

        def round_items(r):
            return [(kind, hc) for hc in (2 * r, 2 * r + 1) for kind in "qk"]

        v_items = [("v", s, half) for s in range(STACKS) for half in range(2)]
        items = round_items(0) + round_items(1) + v_items + round_items(2) + round_items(3)
        item_at = {it: i for i, it in enumerate(items)}
        piece_order = [0, 2, 4, 5, 1, 3]

        def piece_of(it):
            if it[0] == "v":
                return 4 + it[2]
            return (0 if it[0] == "q" else 2) + it[1] // 4

        def moving(x, kc):
            return x[:, kc, :].rearrange("p (g t) -> p g t", t=32)[:, 0:GROUPS, 0:GT]

        def product(pe, dst, pairs):
            for i, ((w_hi, w_lo), (x_hi, x_lo)) in enumerate(pairs):
                pe.matmul(dst, w_hi, x_hi, start=(i == 0), stop=False)
                pe.matmul(dst, w_hi, x_lo, start=False, stop=False)
                last = pe.matmul(dst, w_lo, x_hi, start=False, stop=(i == len(pairs) - 1))
            return last

        def att_copies(dst, r):
            d = dst[:, 2 * r:2 * r + 2, :].rearrange("p c (s q i) -> p q (c s) i", q=Q4, i=32)
            a = ps[:, PROJ_BANK:PROJ_BANK + Q4, 0:SCOLS].rearrange("p q (c t) -> p q c t", t=GT)
            d3 = dst[:, 2 * r:2 * r + 2, :].rearrange("p c (s q i) -> p q c s i", q=Q4, i=32)[:, 3, :, 0:2, 0:GT]
            a3 = ps[:, PROJ_BANK + 3, 0:SCOLS].rearrange("p (c s t) -> p c s t", s=STACKS, t=GT)[:, :, 0:2, :]
            return [(d[:, 0:3, :, 0:GT], a[:, 0:3]), (d3, a3)]

        block = ctx.enter_context(nc.Block())

        @block.sync
        def _(sp):
            sp.dma_start(xw_s[:], xw).then_inc(ld_x, 16)
            sp.dma_start(w1_s[:], w1).then_inc(ld_x, 16)
            sp.dma_start(cols_s[:], bias_cols).then_inc(ld_x, 16)
            for dst, src in ((freq_s, freqs), (tcol_s, tcol), (phase_s, phase), (sign_s, sign)):
                sp.dma_start(dst[:], src).then_inc(ld_rope, 16)
            sp.dma_start(w2_s[:], w2).then_inc(ld_w2, 16)
            sp.dma_start(w3_s[:], w3).then_inc(ld_w3, 16)
            sp.dma_start(w4_s[:], w4).then_inc(ld_w45, 16)
            sp.dma_start(w5_s[:], w5).then_inc(ld_w45, 16)
            sp.dma_start(b5_s[:], b5).then_inc(ld_w45, 16)
            sp.dma_start(rows_s[:].rearrange("p a b -> p (a b)"), rows.broadcast_to([P, 4 * DIM])).then_inc(ld_rows, 16)
            sp.dma_start(ident_s[:], ident).then_inc(ld_misc, 16)
            sp.dma_start(maskq_f[:], mask_q).then_inc(ld_misc, 16)
            sp.dma_start(maskk_f[:], mask_k).then_inc(ld_misc, 16)
            sp.dma_start(gate_s[:], w_gate.rearrange("(k p) e -> p k e", p=P)).then_inc(ld_misc, 16)
            qkv_v = w_qkv.rearrange("(k p) n -> p k n", p=P)
            for i in piece_order:
                sp.dma_start(qkv_raw[:, :, BANK * i:BANK * (i + 1)], qkv_v[:, :, BANK * i:BANK * (i + 1)])\
                  .then_inc(ld_qkv[i], 16)
            sp.wait_ge(conv5_mm, STACKS)
            for j in range(EXPERTS + 1):
                slot = j % RAW_SLOTS
                if j >= RAW_SLOTS:
                    sp.wait_ge(raw_high, j - RAW_SLOTS + 1)
                    sp.wait_ge(raw_low, j - RAW_SLOTS + 1)
                if j == 0:
                    sp.dma_start(raw[:, slot, :].rearrange("p (k d) -> p k d", k=HC),
                                 w_out.rearrange("(k p) d -> p k d", p=P)).then_inc(ld_raw[slot], 32)
                    continue
                e = j - 1
                sp.dma_start(raw[:, slot, 0:KC * HIDDEN].rearrange("p (k n) -> p k n", k=KC),
                             W1[e].rearrange("(k p) n -> p k n", p=P)).then_inc(ld_raw[slot], 16)
                sp.dma_start(raw[:, slot, KC * HIDDEN:].rearrange("p (k n) -> p k n", k=HK),
                             W2[e].rearrange("(k p) n -> p k n", p=P)).then_inc(ld_raw[slot], 16)
            out_rows = out.rearrange("b t d -> (b t) d")
            for s in range(STACKS):
                sp.wait_ge(mixed, STACKS * (EXPERTS - 1) + s + 1)
                for q in range(Q4):
                    g = Q4 * s + q
                    n = min(GT, CLIPS * FRAMES - GT * g)
                    if n > 0:
                        sp.dma_start(out_rows[GT * g:GT * g + n, :], h[32 * q:32 * q + n, s, :]).then_inc(stored, 16)
            sp.wait_ge(stored, 16 * GROUPS)

        @block.tensor
        def _(pe):
            pe.wait_ge(ld_x, 48)
            for c in range(C_PARTS):
                pe.matmul(ps[:, c, :], w1_s[:], xw_s[:, BANK * c:BANK * (c + 1)], start=True, stop=True)\
                  .then_inc(conv1_mm, 1)
            pe.wait_ge(ld_w2, 16)
            pe.wait_ge(pad_zero, 1)
            pe.wait_ge(end_zero, 1)
            for c in range(C_PARTS):
                pe.wait_ge(conv1_act, c + 1)
                for b in range(2):
                    at = (C1_STEP * c + b) * CLIPS
                    mm = pe.matmul(ps[0:C2, 3 + c, :], w2_s[:, b, :], h1[:, at:at + BANK], start=(b == 0), stop=(b == 1))
                mm.then_inc(conv2_mm, 1)
            pe.wait_ge(ld_w3, 16)
            pe.wait_ge(pad_zero, 3)
            pe.wait_ge(conv2_act, C_PARTS)
            pe.wait_ge(conv2_up, C_PARTS)
            for m in range(KC):
                for j in range(PAIRS):
                    k = P if 2 * j + 1 < K3 else C2
                    x = h2[0:k, 2 * j:2 * j + S3 * (FRAMES - 1) + 1:S3, :]
                    mm = pe.matmul(ps[:, 6 + m, 0:FRAMES * CLIPS], w3_s[0:k, j, P * m:P * (m + 1)], x,
                                   start=(j == 0), stop=(j == PAIRS - 1))
                mm.then_inc(conv3_mm, 1)
            pe.wait_ge(ld_w45, 48)
            for m in range(KC):
                pe.wait_ge(conv3_act, m + 1)
                for j in range(3):
                    mm = pe.matmul(ps[:, m, 0:FRAMES * CLIPS], w4_s[:, m, j, :], h3[:, m, j:j + FRAMES, :],
                                   start=(j == 0), stop=(j == 2))
                mm.then_inc(conv4_mm, 1)
            pe.wait_ge(const_ready, 1)
            for s in range(STACKS):
                pe.matmul(ps[:, 2 + s, 0:DIM], ones_s[:], b5_s[:], start=True, stop=False)
            pe.wait_ge(conv4_act, KC)
            for s in range(STACKS):
                for k in range(KC):
                    mm = pe.matmul(ps[:, 2 + s, 0:DIM], h4[:, k, P * s:P * (s + 1)], w5_s[:, k, :],
                                   start=False, stop=(k == KC - 1))
                mm.then_inc(conv5_mm, 1)

            def turn(n, banks):
                for s in range(STACKS):
                    pe.wait_ge(xn_ready, STACKS * n + s + 1)
                    for k in range(KC):
                        mm = pe.transpose(ps[:, banks[k], P * s:P * (s + 1)], xn[:, s, P * k:P * (k + 1)], ident_s[:])
                mm.then_inc(xT_mm, 1)

            pe.wait_ge(ld_misc, 64)
            turn(0, (5, 6))

            def project(some):
                for it in some:
                    i = item_at[it]
                    piece = piece_order.index(piece_of(it)) + 1
                    pe.wait_ge(qkv_high, piece)
                    pe.wait_ge(qkv_low, piece)
                    if i >= 4:
                        pe.wait_ge(proj_out, i - 3)
                    bank = PROJ_BANK + i % 4
                    if it[0] == "v":
                        _, s, half = it
                        at = 2 * INNER + half * BANK
                        mm = product(pe, ps[:, bank, :],
                                     [((xT_hi[:, k, P * s:P * (s + 1)], xT_lo[:, k, P * s:P * (s + 1)]),
                                       (qkv_hi[:, k, at:at + BANK], qkv_lo[:, k, at:at + BANK])) for k in range(KC)])
                    else:
                        at = (0 if it[0] == "q" else INNER) + it[1] * P
                        mm = product(pe, ps[:, bank, 0:TOK],
                                     [((qkv_hi[:, k, at:at + P], qkv_lo[:, k, at:at + P]),
                                       (moving(xT_hi, k), moving(xT_lo, k))) for k in range(KC)])
                    mm.then_inc(proj_mm, 1)

            def scores(r):
                pe.wait_ge(proj_out, item_at[("k", 2 * r + 1)] + 1)
                if r >= 1:
                    pe.wait_ge(s_shift, r)
                for b in range(Q4):
                    pe.matmul(ps[:, b, 0:SCOLS], maskq_s[32 * b:32 * b + GROUP_CLIPS, :],
                              maskk_s[32 * b:32 * b + GROUP_CLIPS, :], start=True, stop=True)
                for hcl in range(2):
                    buf = 2 * r + hcl
                    for g in range(GROUPS):
                        s, q = divmod(g, Q4)
                        at = (STACKS * hcl + s) * GT
                        for b in range(Q4):
                            rows_ = slice(32 * b, 32 * b + 32)
                            mm = pe.matmul(ps[32 * q:32 * q + GT, b, at:at + GT], qT[rows_, buf, GT * g:GT * (g + 1)],
                                           kT[rows_, buf, GT * g:GT * (g + 1)], start=False, stop=True,
                                           skip_group_check=True)
                mm.then_inc(score_mm, 1)

            def pv(r):
                pe.wait_ge(s_turn, r + 1)
                if r >= 1:
                    pe.wait_ge(att_high, 2 * r)
                    pe.wait_ge(att_low, 2 * r)
                for hcl in range(2):
                    for s in range(STACKS):
                        at = (STACKS * hcl + s) * GT
                        for b in range(Q4):
                            head = 4 * (2 * r + hcl) + b
                            for q in range(Q4):
                                if Q4 * s + q >= GROUPS:
                                    continue
                                mm = pe.matmul(ps[32 * b:32 * b + 32, PROJ_BANK + q, at:at + GT],
                                               v_s[32 * q:32 * q + GT, s, 32 * head:32 * head + 32],
                                               probT[32 * q:32 * q + GT, r % 2, COMBOS * b + STACKS * hcl + s, 0:GT],
                                               start=True, stop=True)
                mm.then_inc(pv_mm, 1)

            def out_project(r):
                pe.wait_ge(att_high, 2 * r + 2)
                pe.wait_ge(att_low, 2 * r + 2)
                for s in range(STACKS):
                    for hc in (2 * r, 2 * r + 1):
                        a = slice(P * s, P * (s + 1))
                        dst = ps[:, s, 0:DIM]
                        pe.matmul(dst, att_hi[:, hc, a], wout_hi[:, hc, :], start=(hc == 0), stop=False)
                        pe.matmul(dst, att_hi[:, hc, a], wout_lo[:, hc, :], start=False, stop=False)
                        mm = pe.matmul(dst, att_lo[:, hc, a], wout_hi[:, hc, :], start=False, stop=(hc == HC - 1))
                    if r == ROUNDS - 1:
                        mm.then_inc(out_mm, 1)

            pe.wait_ge(xT_high, 1)
            pe.wait_ge(xT_low, 1)
            pe.wait_ge(const_ready, 2)
            project(round_items(0))
            scores(0)
            project(round_items(1))
            project(v_items)
            project(round_items(2))
            scores(1)
            project(round_items(3))
            scores(2)
            pe.wait_ge(proj_out, len(items))
            pv(0)
            scores(3)
            pv(1)
            pe.wait_ge(s_shift, ROUNDS)
            pe.wait_ge(raw_high, 1)
            pe.wait_ge(raw_low, 1)
            out_project(0)
            pv(2)
            out_project(1)
            pv(3)
            out_project(2)
            out_project(3)

            turn(1, (7, 3))

            def up(e):
                pe.wait_ge(raw_high, e + 2)
                pe.wait_ge(raw_low, e + 2)
                slot = e % SPLIT_SLOTS
                for m in range(HK):
                    n = HK * e + m
                    if n >= 4:
                        pe.wait_ge(relu_done, n - 3)
                    pairs = []
                    for k in range(KC):
                        at = k * HIDDEN + P * m
                        pairs.append(((exp_hi[:, slot, at:at + P], exp_lo[:, slot, at:at + P]),
                                      (moving(xT_hi, k), moving(xT_lo, k))))
                    product(pe, ps[:, n % 4, 0:TOK], pairs).then_inc(up_mm, 1)

            def down(e):
                pe.wait_ge(hid_high, HK * (e + 1))
                pe.wait_ge(hid_low, HK * (e + 1))
                if e >= 2:
                    pe.wait_ge(mixed, STACKS * (e - 1))
                slot = e % SPLIT_SLOTS
                for s in range(STACKS):
                    dst = ps[:, 4 + 2 * (e % 2) + s // 2, DIM * (s % 2):DIM * (s % 2) + DIM]
                    pairs = []
                    for k in range(HK):
                        at = KC * HIDDEN + k * DIM
                        n = HK * (e % 2) + k
                        pairs.append(((hid_hi[:, n, P * s:P * (s + 1)], hid_lo[:, n, P * s:P * (s + 1)]),
                                      (exp_hi[:, slot, at:at + DIM], exp_lo[:, slot, at:at + DIM])))
                    product(pe, dst, pairs).then_inc(down_mm, 1)

            pe.wait_ge(xT_high, 2)
            pe.wait_ge(xT_low, 2)
            up(0)
            pe.wait_ge(xT_full, 1)
            for s in range(STACKS):
                for k in range(KC):
                    mm = pe.matmul(ps[:, 7, EXPERTS * s:EXPERTS * (s + 1)], xT_f[:, k, P * s:P * (s + 1)],
                                   gate_s[:, k, :], start=(k == 0), stop=(k == KC - 1))
            mm.then_inc(gate_mm, 1)
            for e in range(EXPERTS):
                if e + 1 < EXPERTS:
                    up(e + 1)
                if e == 1:
                    pe.wait_ge(g_step, 1)
                down(e)

        @block.scalar
        def _(act):
            act.wait_ge(angle, 8)
            act.activation(table[:], ang[:, 5, :], ACT.Sin).then_inc(sines, 1)

            b1 = cols_s[:, COL_B1:COL_B1 + 1]
            for c in range(C_PARTS):
                act.wait_ge(conv1_mm, c + 1)
                at, n = (C1_STEP * c + 1) * CLIPS, BANK
                if c == C_PARTS - 1:
                    n = BANK - CLIPS
                    act.activation(h1[0:64, at + n:at + BANK], ps[0:64, c, n:BANK], ACT.Gelu, bias=b1[0:64, :])
                act.activation(h1[:, at:at + n], ps[:, c, 0:n], ACT.Gelu, bias=b1).then_inc(conv1_act, 1)
            act.wait_ge(pad_zero, 2)
            for c in range(C_PARTS):
                act.wait_ge(conv2_mm, c + 1)
                at = PAD3 + C1_STEP * c
                act.activation(h2[0:C2, at:at + C1_STEP, :].rearrange("p a b -> p (a b)"), ps[0:C2, 3 + c, :], ACT.Gelu,
                               bias=cols_s[0:C2, COL_B2:COL_B2 + 1]).then_inc(conv2_act, 1)
            for m in range(KC):
                act.wait_ge(conv3_mm, m + 1)
                act.activation(h3[:, m, 1:1 + FRAMES, :].rearrange("p a b -> p (a b)"), ps[:, 6 + m, 0:FRAMES * CLIPS],
                               ACT.Gelu, bias=cols_s[:, COL_B3 + m:COL_B3 + m + 1]).then_inc(conv3_act, 1)
            act.wait_ge(pad_zero, 4)
            for m in range(KC):
                act.wait_ge(conv4_mm, m + 1)
                bias = cols_s[:, COL_B4 + m:COL_B4 + m + 1]
                src = ps[:, m, 0:FRAMES * CLIPS].rearrange("p (t b) -> p b t", t=FRAMES)
                dst = h4[:, m, :].rearrange("p (g i) -> p g i", i=32)
                full = FULL_GROUPS * GROUP_CLIPS
                act.activation(dst[:, 0:FULL_GROUPS, 0:GT].rearrange("p g (b t) -> p g b t", t=FRAMES),
                               src[:, 0:full, :].rearrange("p (g b) t -> p g b t", b=GROUP_CLIPS), ACT.Gelu, bias=bias)
                act.activation(dst[:, FULL_GROUPS, 0:REST_CLIPS * FRAMES].rearrange("p (b t) -> p b t", t=FRAMES),
                               src[:, full:CLIPS, :], ACT.Gelu, bias=bias).then_inc(conv4_act, 1)
            for s in range(STACKS):
                act.wait_ge(conv5_mm, s + 1)
                act.activation(x5[:, s, :], ps[:, 2 + s, 0:DIM], ACT.Gelu).then_inc(conv5_act, 1)
            for s in range(STACKS):
                act.wait_ge(rope_y, s + 1)
                act.activation(xn[:, s, :], ropa[:, s, :], ACT.Square, accum_out=ssq[:, s:s + 1]).then_inc(squares, 1)

            def turned(n, banks):
                act.wait_ge(xT_mm, n + 1)
                for k in range(KC):
                    cp = act.activation(xT_hi[:, k, :], ps[:, banks[k], 0:SLOTS], ACT.Copy)
                cp.then_inc(xT_high, 1)

            turned(0, (5, 6))

            def copy_out(some):
                for it in some:
                    i = item_at[it]
                    act.wait_ge(proj_mm, i + 1)
                    bank = PROJ_BANK + i % 4
                    if it[0] == "v":
                        dst, src = v_s[:, it[1], BANK * it[2]:BANK * (it[2] + 1)], ps[:, bank, :]
                    else:
                        dst, src = (qT if it[0] == "q" else kT)[:, it[1], :], ps[:, bank, 0:TOK]
                    act.activation(dst, src, ACT.Copy).then_inc(proj_out, 1)

            def exponentials(r):
                act.wait_ge(s_shift, r + 1)
                act.activation(prob[:, :, 0:GT], prob[:, :, 0:GT], ACT.Exp, scale=SCALE).then_inc(s_exp, 1)

            def attended(r):
                act.wait_ge(pv_mm, r + 1)
                act.wait_ge(att_zero, 1)
                for dst, src in att_copies(att_hi, r):
                    act.activation(dst, src, ACT.Copy).then_inc(att_high, 1)

            def split(j):
                act.wait_ge(ld_raw[j % RAW_SLOTS], 32 * (j // RAW_SLOTS + 1))
                if j >= 1:
                    if j <= SPLIT_SLOTS:
                        act.wait_ge(proj_mm, len(items))
                    else:
                        act.wait_ge(down_mm, STACKS * (j - SPLIT_SLOTS))
                dst = wout_hi[:].rearrange("p k d -> p (k d)") if j == 0 else exp_hi[:, (j - 1) % SPLIT_SLOTS, :]
                act.activation(dst, raw[:, j % RAW_SLOTS, :], ACT.Copy).then_inc(raw_high, 1)

            copy_out(round_items(0))
            copy_out(round_items(1))
            exponentials(0)
            copy_out(v_items)
            copy_out(round_items(2))
            exponentials(1)
            copy_out(round_items(3))
            split(0)
            exponentials(2)
            attended(0)
            exponentials(3)
            attended(1)
            split(1)
            attended(2)
            split(2)
            attended(3)
            split(3)

            turned(1, (7, 3))

            for e in range(EXPERTS):
                for m in range(HK):
                    n = HK * e + m
                    act.wait_ge(up_mm, n + 1)
                    if n >= 2:
                        act.wait_ge(sq_done, n - 1)
                        act.wait_ge(hid_high, n - 1)
                    act.activation(relu[:, n % 2, :], ps[:, n % 4, 0:TOK], ACT.Relu).then_inc(relu_done, 1)
                    act.wait_ge(relu_done, n + 1)
                    if e >= 2:
                        act.wait_ge(down_mm, STACKS * (e - 1))
                    if n == 0:
                        act.wait_ge(pad_zero, 5)
                    dst = hid_hi[:, n % (2 * HK), :].rearrange("p (g t) -> p g t", t=32)[:, 0:GROUPS, 0:GT]
                    act.activation(dst, relu[:, n % 2, :].rearrange("p (g t) -> p g t", t=GT), ACT.Square)\
                       .then_inc(hid_high, 1)
                if e == 0:
                    act.wait_ge(g_step, 3)
                    act.activation(logit[:], logit[:], ACT.Exp).then_inc(g_exp, 1)
                if e >= 1 and e + 3 <= EXPERTS:
                    split(e + 3)

        @block.gpsimd
        def _(pool):
            pool.memset(h1[:, 0:CLIPS], 0.0).then_inc(pad_zero, 1)
            pool.memset(h2[:, 0:PAD3, :], 0.0)
            pool.memset(h2[:, PAD3 + L2 - 1:, :], 0.0).then_inc(pad_zero, 1)
            pool.memset(h3[:, :, 0:FRAMES + 2:FRAMES + 1, :], 0.0).then_inc(pad_zero, 1)
            pool.memset(h4[:], 0.0).then_inc(pad_zero, 1)
            pool.memset(ones_s[:], 1.0).then_inc(const_ready, 1)
            pool.memset(power[:], -0.5)
            pool.memset(gprob[:], -1.0)
            pool.memset(gfind[:], -1.0)
            pool.memset(prob[:], 0.0)
            pool.wait_ge(ld_misc, 64)
            pool.tensor_copy(maskq_s[:], maskq_f[:])
            pool.tensor_copy(maskk_s[:], maskk_f[:]).then_inc(const_ready, 1)

            def inverse_root(n, src, scale, eps):
                pool.tensor_scalar(var[:], src, scale, eps, ALU.mult, ALU.add).then_inc(rstd_var, 1)
                pool.wait_ge(rstd_var, n + 1)
                pool.tensor_tensor(rstd[:, n, :], var[:], power[:], ALU.pow).then_inc(rstd_ready, 1)

            pool.wait_ge(squares, STACKS)
            inverse_root(0, ssq[:], 1.0 / DIM, RMS_EPS)
            pool.wait_ge(mv_ready, STACKS)
            inverse_root(1, mv[:, 0, :, 1], 1.0, LN_EPS)
            pool.wait_ge(qkv_low, 6)
            pool.memset(att_hi[:].bitcast(F32), 0.0)
            pool.memset(att_lo[:].bitcast(F32), 0.0).then_inc(att_zero, 1)
            pool.wait_ge(ld_rows, 16)
            pool.wait_ge(xn_ready, STACKS)
            for s in range(STACKS):
                pool.tensor_tensor(ropb[:, s, :], h[:, s, :], rows_s[:, ROW_BETA, :], ALU.add).then_inc(hb_ready, 1)
            pool.wait_ge(pv_mm, ROUNDS)
            pool.memset(hid_hi[:].bitcast(F32), 0.0)
            pool.memset(hid_lo[:].bitcast(F32), 0.0).then_inc(pad_zero, 1)
            pool.wait_ge(mv_ready, 2 * STACKS)
            inverse_root(2, mv[:, 1, :, 1], 1.0, ATT_EPS)
            pool.wait_ge(mv_ready, 3 * STACKS)
            inverse_root(3, mv[:, 2, :, 1], 1.0, LN_EPS)
            pool.wait_ge(xT_low, 2)
            pool.tensor_tensor(xT_f, xT_hi[:].bitcast(F32), xT_lo[:].bitcast(F32), ALU.add).then_inc(xT_full, 1)
            for n in range(HK * EXPERTS):
                pool.wait_ge(relu_done, n + 1)
                if n >= 2:
                    pool.wait_ge(hid_low, n - 1)
                pool.tensor_tensor(sq[:, n % 2, :], relu[:, n % 2, :], relu[:, n % 2, :], ALU.mult).then_inc(sq_done, 1)

        @block.vector
        def _(dve):
            dve.memset(h1[64:P, BLOCKS * CLIPS:], 0.0).then_inc(end_zero, 1)
            dve.wait_ge(ld_rope, 64)
            n_angle = [0]

            def angle_step(ins):
                n_angle[0] += 1
                ins.then_inc(angle, 1)
                dve.wait_ge(angle, n_angle[0])

            angle_step(dve.tensor_scalar(ang[:, 0, :], freq_s[:], tcol_s[:], None, ALU.mult))
            angle_step(dve.tensor_tensor(ang[:, 1, :], ang[:, 0, :], phase_s[:], ALU.add))
            angle_step(dve.tensor_scalar(ang[:, 2, :], ang[:, 1, :], 1.0 / (2 * PI), ROUNDER, ALU.mult, ALU.add))
            angle_step(dve.tensor_scalar(ang[:, 2, :], ang[:, 2, :], ROUNDER, None, ALU.subtract))
            angle_step(dve.scalar_tensor_tensor(out=ang[:, 3, :], in0=ang[:, 2, :], scalar=-TWO_PI_HI, in1=ang[:, 0, :],
                                                op0=ALU.mult, op1=ALU.add))
            angle_step(dve.scalar_tensor_tensor(out=ang[:, 4, :], in0=ang[:, 2, :], scalar=-TWO_PI_MID, in1=ang[:, 3, :],
                                                op0=ALU.mult, op1=ALU.add))
            angle_step(dve.tensor_tensor(ang[:, 3, :], ang[:, 4, :], phase_s[:], ALU.add))
            angle_step(dve.tensor_scalar(ang[:, 5, :], ang[:, 3, :], 3.1415925, -3.1415925, ALU.min, ALU.max))
            dve.wait_ge(sines, 1)
            dve.tensor_tensor(table[:], table[:], sign_s[:], ALU.mult).then_inc(table_ready, 1)

            dve.wait_ge(pad_zero, 2)
            for c in range(C_PARTS):
                dve.wait_ge(conv2_act, c + 1)
                at = PAD3 + C1_STEP * c
                dve.tensor_copy(h2[C2:P, at - 1:at - 1 + C1_STEP, :], h2[0:C2, at:at + C1_STEP, :]).then_inc(conv2_up, 1)

            for n, i in enumerate(piece_order):
                a = slice(BANK * i, BANK * (i + 1))
                dve.wait_ge(ld_qkv[i], 16)
                dve.tensor_copy(qkv_hi[:, :, a], qkv_raw[:, :, a]).then_inc(qkv_high, 1)
                dve.wait_ge(qkv_high, n + 1)
                dve.tensor_tensor(qkv_lo[:, :, a], qkv_raw[:, :, a], qkv_hi[:, :, a].bitcast(F32), ALU.subtract)\
                   .then_inc(qkv_low, 1)

            dve.wait_ge(table_ready, 1)
            cos_b = table[:, None, 0:16].broadcast_to([P, 16, 16])
            sin_b = table[:, None, 16:32].broadcast_to([P, 16, 16])
            for s in range(STACKS):
                dve.wait_ge(conv5_act, s + 1)
                x = x5[:, s, :].rearrange("p (h d) -> p h d", d=16)
                a = ropa[:, s, :].rearrange("p (h d) -> p h d", d=16)
                b = ropb[:, s, :].rearrange("p (h d) -> p h d", d=16)
                dve.tensor_tensor(a, x, cos_b, ALU.mult).then_inc(rope_a, 1)
                for i in range(2):
                    dve.tensor_tensor(b[:, :, i::2], x[:, :, 1 - i::2], sin_b[:, :, i::2], ALU.mult).then_inc(rope_b, 1)
            for s in range(STACKS):
                dve.wait_ge(rope_a, s + 1)
                dve.wait_ge(rope_b, 2 * s + 2)
                dve.tensor_tensor(ropa[:, s, :], ropa[:, s, :], ropb[:, s, :], ALU.add).then_inc(rope_y, 1)
            dve.wait_ge(ld_rows, 16)
            dve.wait_ge(rstd_ready, 1)
            dve.wait_ge(rope_y, STACKS)
            for s in range(STACKS):
                dve.scalar_tensor_tensor(out=h[:, s, :], in0=ropa[:, s, :], scalar=rstd[:, 0, s:s + 1],
                                         in1=rows_s[:, ROW_NORM, :], op0=ALU.mult, op1=ALU.mult).then_inc(h_ready, 1)

            def moments(n, src, ready, base):
                for s in range(STACKS):
                    dve.wait_ge(ready, base + s + 1)
                    dve.bn_stats(stats[:, s, :], src[:, s, :]).then_inc(stat_ready, 1)
                for s in range(STACKS):
                    dve.wait_ge(stat_ready, STACKS * n + s + 1)
                    dve.bn_aggr(mv[:, n, s, :], stats[:, s, :]).then_inc(mv_ready, 1)

            def normalize(n, dst, src, root, done):
                dve.wait_ge(rstd_ready, root + 1)
                dve.wait_ge(mv_ready, STACKS * (n + 1))
                for s in range(STACKS):
                    dve.tensor_scalar(dst[:, s, :], src[:, s, :], mv[:, n, s, 0:1], rstd[:, root, s:s + 1],
                                      ALU.subtract, ALU.mult).then_inc(done, 1)

            def turned(n, banks):
                dve.wait_ge(xT_high, n + 1)
                for k in range(KC):
                    sub = dve.tensor_tensor(xT_lo[:, k, :], ps[:, banks[k], 0:SLOTS], xT_hi[:, k, :].bitcast(F32),
                                            ALU.subtract)
                sub.then_inc(xT_low, 1)

            moments(0, h, h_ready, 0)
            normalize(0, xn, h, 1, xn_ready)
            turned(0, (5, 6))

            def shift(r):
                dve.wait_ge(score_mm, r + 1)
                if r >= 1:
                    dve.wait_ge(s_turn, r)
                src = ps[:, 0:Q4, 0:SCOLS].rearrange("p b (c t) -> p b c t", t=GT)
                top = smax[:].rearrange("p (b c) -> p b c", b=Q4)
                dve.tensor_reduce(top, src, AX.X, ALU.max).then_inc(s_max, 1)
                dve.wait_ge(s_max, r + 1)
                dst = prob[:].rearrange("p (b c) t -> p b c t", b=Q4)[:, :, :, 0:GT]
                dve.tensor_tensor(dst, src, top[:, :, :, None].broadcast_to([P, Q4, COMBOS, GT]), ALU.subtract)\
                   .then_inc(s_shift, 1)

            def finish_softmax(r):
                dve.wait_ge(s_exp, r + 1)
                e = prob[:, :, 0:GT]
                dve.tensor_reduce(ssum[:], e, AX.X, ALU.add).then_inc(s_sum, 1)
                dve.wait_ge(s_sum, r + 1)
                dve.reciprocal(ssum[:], ssum[:]).then_inc(s_inv, 1)
                dve.wait_ge(s_inv, r + 1)
                dve.tensor_tensor(e, e, ssum[:, :, None].broadcast_to([P, Q4 * COMBOS, GT]), ALU.mult).then_inc(s_norm, 1)
                dve.wait_ge(s_norm, r + 1)
                if r >= 2:
                    dve.wait_ge(pv_mm, r - 1)
                dve.transpose(probT[:, r % 2].rearrange("p c t -> p (c t)"), prob[:].rearrange("p c t -> p (c t)"))\
                   .then_inc(s_turn, 1)

            def attended(r):
                for n, ((dst, src), (hi, _)) in enumerate(zip(att_copies(att_lo, r), att_copies(att_hi, r))):
                    dve.wait_ge(att_high, 2 * r + n + 1)
                    dve.tensor_tensor(dst, src, hi.bitcast(F32), ALU.subtract).then_inc(att_low, 1)

            def split(j):
                dve.wait_ge(raw_high, j + 1)
                if j == 0:
                    dst, hi = wout_lo[:].rearrange("p k d -> p (k d)"), wout_hi[:].rearrange("p k d -> p (k d)")
                else:
                    dst, hi = exp_lo[:, (j - 1) % SPLIT_SLOTS, :], exp_hi[:, (j - 1) % SPLIT_SLOTS, :]
                dve.tensor_tensor(dst, raw[:, j % RAW_SLOTS, :], hi.bitcast(F32), ALU.subtract).then_inc(raw_low, 1)

            shift(0)
            finish_softmax(0)
            shift(1)
            finish_softmax(1)
            split(0)
            shift(2)
            finish_softmax(2)
            attended(0)
            shift(3)
            finish_softmax(3)
            attended(1)
            split(1)
            attended(2)
            split(2)
            attended(3)
            split(3)

            for s in range(STACKS):
                dve.wait_ge(out_mm, s + 1)
                dve.tensor_tensor(x5[:, s, :], ps[:, s, 0:DIM], rows_s[:, ROW_BOUT, :], ALU.add)\
                   .then_inc(out_bias, 1)
            moments(1, x5, out_bias, 0)
            normalize(1, x5, x5, 2, ln_z)
            dve.wait_ge(hb_ready, STACKS)
            for s in range(STACKS):
                dve.wait_ge(ln_z, s + 1)
                dve.tensor_tensor(ropa[:, s, :], x5[:, s, :], rows_s[:, ROW_GAMMA, :], ALU.mult).then_inc(ln_zg, 1)
            for s in range(STACKS):
                dve.wait_ge(ln_zg, s + 1)
                dve.tensor_tensor(h[:, s, :], ropa[:, s, :], ropb[:, s, :], ALU.add).then_inc(h_ready, 1)
            moments(2, h, h_ready, STACKS)
            normalize(2, xn, h, 3, xn_ready)
            turned(1, (7, 3))

            def gate():
                n_gate = [0]

                def step(ins):
                    n_gate[0] += 1
                    ins.then_inc(g_step, 1)
                    dve.wait_ge(g_step, n_gate[0])

                def wide(x):
                    return x[:, :, None].broadcast_to([P, STACKS, EXPERTS])

                dve.wait_ge(gate_mm, 1)
                step(dve.tensor_copy(logit[:].rearrange("p s e -> p (s e)"), ps[:, 7, 0:STACKS * EXPERTS]))
                step(dve.tensor_reduce(gmax[:], logit[:], AX.X, ALU.max))
                step(dve.tensor_tensor(logit[:], logit[:], wide(gmax), ALU.subtract))
                dve.wait_ge(g_exp, 1)
                step(dve.tensor_reduce(gsum[:], logit[:], AX.X, ALU.add))
                step(dve.reciprocal(gsum[:], gsum[:]))
                probs = gprob[:, :, 0:EXPERTS]
                step(dve.tensor_tensor(probs, logit[:], wide(gsum), ALU.mult))
                for s in range(STACKS):
                    step(dve.max(gtop[:, s, :], gprob[:, s, 0:EXPERTS]))
                step(dve.tensor_copy(gfind[:, :, 0:2], gtop[:, :, 0:2]))
                for s in range(STACKS):
                    step(dve.match_replace(gleft[:, s, :], gfind[:, s, :], gprob[:, s, :], -2.0))
                step(dve.tensor_tensor(comb[:], gleft[:, :, 0:EXPERTS], probs, ALU.not_equal))
                step(dve.tensor_tensor(comb[:], comb[:], probs, ALU.mult))
                step(dve.tensor_tensor(gsum[:], gtop[:, :, 0], gtop[:, :, 1], ALU.add))
                step(dve.tensor_scalar(gsum[:], gsum[:], TOP_EPS, None, ALU.add))
                step(dve.reciprocal(gsum[:], gsum[:]))
                dve.tensor_tensor(comb[:], comb[:], wide(gsum), ALU.mult).then_inc(comb_ready, 1)

            def low_parts(e):
                for m in range(HK):
                    n = HK * e + m
                    dve.wait_ge(sq_done, n + 1)
                    dve.wait_ge(hid_high, n + 1)
                    if n == 0:
                        dve.wait_ge(pad_zero, 5)
                    hi, lo = (x[:, n % (2 * HK), :].rearrange("p (g t) -> p g t", t=32)[:, 0:GROUPS, 0:GT]
                              for x in (hid_hi, hid_lo))
                    dve.tensor_tensor(lo, sq[:, n % 2, :].rearrange("p (g t) -> p g t", t=GT), hi.bitcast(F32),
                                      ALU.subtract).then_inc(hid_low, 1)

            def mix(e):
                for s in range(STACKS):
                    dve.wait_ge(down_mm, STACKS * e + max(s, 1) + 1)
                    if e:
                        dve.wait_ge(mixed, STACKS * (e - 1) + s + 1)
                    src = ps[:, 4 + 2 * (e % 2) + s // 2, DIM * (s % 2):DIM * (s % 2) + DIM]
                    dve.scalar_tensor_tensor(out=h[:, s, :], in0=src, scalar=comb[:, s, e:e + 1], in1=h[:, s, :],
                                             op0=ALU.mult, op1=ALU.add).then_inc(mixed, 1)

            low_parts(0)
            gate()
            dve.wait_ge(comb_ready, 1)
            for e in range(EXPERTS):
                if e + 1 < EXPERTS:
                    low_parts(e + 1)
                if e >= 1 and e + 3 <= EXPERTS:
                    split(e + 3)
                mix(e)


_OUT = ((CLIPS, FRAMES, DIM), "float32")


def kernel(**inputs):
    import numpy as np
    import concourse.bacc as bacc
    from concourse.bass_utils import run_bass_kernel_spmd

    a = {k: np.ascontiguousarray(v) for k, v in inputs.items()}
    f = np.float32
    arrays = {}
    x = a["x"][:, 0, :]
    padded = np.zeros((CLIPS, PER * S1 * (BLOCKS - 1) + WINDOW + PAD1), f)
    padded[:, PAD1:PAD1 + x.shape[1]] = x
    arrays["xw"] = np.stack([padded[:, PER * S1 * w:PER * S1 * w + WINDOW].T for w in range(BLOCKS)], 1)\
        .reshape(WINDOW, BLOCKS * CLIPS)
    w = np.zeros((WINDOW, PER, C1), f)
    for i in range(PER):
        w[S1 * i:S1 * i + K1, i, :] = a["L0_tok_w1"][:, 0, :].T
    arrays["w1"] = w.reshape(WINDOW, P)
    w = np.zeros((2, PER, C1, C2), f)
    for j in range(K2):
        at = PER - PAD2 + j
        w[at // PER, at % PER] = a["L0_tok_w2"][:, :, j].T
    arrays["w2"] = w.reshape(2, P, C2).transpose(1, 0, 2)
    w = np.zeros((2 * PAIRS, C2, C3), f)
    w[:K3] = a["L0_tok_w3"].transpose(2, 1, 0)
    arrays["w3"] = w.reshape(PAIRS, P, C3).transpose(1, 0, 2)
    w = np.zeros((P, KC, 3, P), f)
    per_group = a["L0_tok_w4"].shape[1]
    for o in range(DIM):
        first = o % P // per_group * per_group
        w[first:first + per_group, o // P, :, o % P] = a["L0_tok_w4"][o]
    arrays["w4"] = w
    arrays["w5"] = a["L0_tok_w5"][:, :, 0].T.reshape(KC, P, DIM).transpose(1, 0, 2)
    cols = np.zeros((P, 6), f)
    cols[:, COL_B1] = np.tile(a["L0_tok_b1"], PER)
    cols[:C2, COL_B2] = a["L0_tok_b2"]
    cols[:, COL_B3:COL_B3 + 2] = a["L0_tok_b3"].reshape(KC, P).T
    cols[:, COL_B4:COL_B4 + 2] = a["L0_tok_b4"].reshape(KC, P).T
    arrays["bias_cols"] = cols
    arrays["b5"] = a["L0_tok_b5"].reshape(1, DIM)
    arrays["rows"] = np.concatenate([a[k] for k in ("L0_tok_norm_w", "L0_attn_b_out", "L0_attn_ln_gamma",
                                                    "L0_attn_ln_beta")]).reshape(1, 4 * DIM)
    pair = np.repeat(a["L0_tok_rope_freqs"], 2)
    arrays["freqs"] = np.ascontiguousarray(np.broadcast_to(np.concatenate([pair, pair]), (P, 32)))
    arrays["w_qkv"] = a["L0_attn_w_qkv"]
    arrays["w_out"] = a["L0_attn_w_out"]
    arrays["w_gate"] = a["L0_ffn_Wg"]
    arrays["W1"] = a["L0_ffn_W1"]
    arrays["W2"] = a["L0_ffn_W2"]
    slot = np.arange(P)
    arrays["tcol"] = (slot % 32 % FRAMES).astype(f).reshape(P, 1)
    arrays["phase"] = np.tile(np.repeat(np.array([PI / 2, 0.0], f), 16), (P, 1))
    arrays["sign"] = np.tile(np.concatenate([np.ones(16, f), np.tile(np.array([-1.0, 1.0], f), 8)]), (P, 1))
    arrays["ident"] = np.eye(P, dtype=f)
    mask_q, mask_k = np.zeros((P, P), f), np.zeros((P, SCOLS), f)
    for b in range(Q4):
        for c in range(GROUP_CLIPS):
            mask_q[32 * b + c] = (slot % 32 < GT) & (slot % 32 // FRAMES == c)
            mask_k[32 * b + c] = np.where(np.arange(SCOLS) % GT // FRAMES == c, 0.0, -2.0 ** 100)
    arrays["mask_q"], arrays["mask_k"] = mask_q, mask_k

    nc = bacc.Bacc("TRN2", target_bir_lowering=False, num_devices=1)
    sent, args = {}, []
    for name, value in arrays.items():
        sent[f"in_{name}"] = np.ascontiguousarray(value)
        args.append(nc.dram_tensor(f"in_{name}", value.shape, mybir.dt.from_np(value.dtype), kind="ExternalInput").ap())
    out = nc.dram_tensor("out_tokens", _OUT[0], mybir.dt.from_np(np.dtype(_OUT[1])), kind="ExternalOutput").ap()
    build(nc, *args, out)
    return run_bass_kernel_spmd(nc, [sent], core_ids=[0]).results[0]["out_tokens"]
```

```python
from contextlib import ExitStack

import concourse.bass as bass
from concourse import mybir

F32 = mybir.dt.float32
F32R = mybir.dt.float32r
BF16 = mybir.dt.bfloat16
ALU = mybir.AluOpType
ACT = mybir.ActivationFunctionType
AX = mybir.AxisListType

P = 128
CLIPS = 64
FRAMES = 5
DIM = 256
KC = DIM // P
HEADS, HEAD_DIM = 32, 32
INNER = HEADS * HEAD_DIM
HC = INNER // P
EXPERTS, HIDDEN = 8, 512
HK = HIDDEN // P
Q4 = 4

GROUP_CLIPS = 6
GT = GROUP_CLIPS * FRAMES
GROUPS = -(-CLIPS // GROUP_CLIPS)
STACKS = -(-GROUPS // Q4)
SLOTS = STACKS * P
TOK = GROUPS * GT
FULL_GROUPS = CLIPS // GROUP_CLIPS
REST_CLIPS = CLIPS - FULL_GROUPS * GROUP_CLIPS

C1, K1, S1, PAD1 = 32, 15, 8, 7
PER = 4
WINDOW = S1 * (PER - 1) + K1
L1 = 94
BLOCKS = 24
C2, K2, PAD2 = 64, 7, 3
L2 = 24
C3, K3, S3, PAD3 = 256, 9, 5, 4
PAIRS = (K3 + 1) // 2
H2_COLS = PAD3 + L2 + 1
BANK = 512
C1_STEP = BANK // CLIPS
C_PARTS = BLOCKS // C1_STEP

PAIR_COUNT = HC // 2
UNITS = STACKS * PAIR_COUNT
DEPTH = 3
SCOLS = 2 * GT
PROJ_BANK = 4
SHARED_PV = 3
OUT_BANK = (7, 7, 0)
TURN_BANK = (3, 2, 7)
UP_BANK = (1, 2, 3, 0)
WARM = (5, 3, 10, 3, 0, 3)
RAW_SLOTS, SPLIT_SLOTS = 4, 3
ECOLS = KC * HIDDEN + HK * DIM
PIECES = 4
PIECE = ECOLS // PIECES

SCALE = float(HEAD_DIM) ** -0.5
PI = 3.14159265358979
TWO_PI_HI, TWO_PI_MID, TWO_PI_LO = 6.28125, 1.9353071693331003e-03, 1.025271e-11
ROUNDER = 12582912.0
LN_EPS, RMS_EPS, ATT_EPS, TOP_EPS = 1e-5, 1e-8, 1e-6, 1e-8

COL_B1, COL_B2, COL_B3, COL_B4, COL_FRAME, COL_FREQ, COL_PHASE, COL_SIGN, SMALL = 0, 1, 2, 4, 6, 7, 39, 71, 103
ROW_NORM, ROW_BOUT, ROW_GAMMA, ROW_BETA, ROW_B5, ROWS = range(6)


def unit_of(u):
    s, p = divmod(u, PAIR_COUNT)
    return s, p, min(Q4, GROUPS - Q4 * s)


def build(nc, xw, small, w2, w3, w45, rows, consts, w_qkv, w_out, W1, W2, out):
    with ExitStack() as ctx:
        def sb(name, shape, dt=F32, life=ctx):
            return life.enter_context(nc.sbuf_tensor(name, shape, dt))

        def sem(name):
            return ctx.enter_context(nc.semaphore(name))

        with ExitStack() as conv:
            xw_s = sb("xw_s", [WINDOW, P + BLOCKS * CLIPS], life=conv)
            w2_s = sb("w2_s", [P, 2, C2], life=conv)
            w3_s = sb("w3_s", [P, PAIRS, C3], life=conv)
            w45_s = sb("w45_s", [P, KC * 3 * P + KC * DIM], life=conv)
            h1 = sb("h1", [P, (BLOCKS + 1) * CLIPS], life=conv)
            h2 = sb("h2", [P, H2_COLS, CLIPS], life=conv)
            h3 = sb("h3", [P, KC, FRAMES + 2, CLIPS], life=conv)
            h4 = sb("h4", [P, KC, SLOTS], life=conv)
        raw = sb("raw", [P, RAW_SLOTS, ECOLS])
        w4_s = w45_s[:, 0:KC * 3 * P].rearrange("p (m j o) -> p m j o", m=KC, j=3)
        w5_s = w45_s[:, KC * 3 * P:].rearrange("p (k o) -> p k o", k=KC)
        sb("conv_rest", [P, 1280])
        with ExitStack() as early:
            qkv_raw = sb("qkv_raw", [P, KC, 3 * INNER], life=early)
        att_hi = sb("att_hi", [P, HC, SLOTS], F32R)
        att_lo = sb("att_lo", [P, HC, SLOTS], F32R)
        with ExitStack() as early:
            qkv_hi = sb("qkv_hi", [P, KC, 3 * INNER], F32R, life=early)
            qkv_lo = sb("qkv_lo", [P, KC, 3 * INNER], F32R, life=early)
        exp_hi = sb("exp_hi", [P, SPLIT_SLOTS, ECOLS], F32R)
        exp_lo = sb("exp_lo", [P, SPLIT_SLOTS, ECOLS], F32R)

        with ExitStack() as early:
            qT = sb("qT", [P, HC, TOK], life=early)
            kT = sb("kT", [P, HC, TOK], life=early)
            v_s = sb("v_s", [P, STACKS, INNER], life=early)
        hid_hi = sb("hid_hi", [P, 2 * HK, SLOTS], F32R)
        hid_lo = sb("hid_lo", [P, 2 * HK, SLOTS], F32R)
        relu = sb("relu", [P, 2, TOK])
        sq = sb("sq", [P, 2, TOK])
        sb("early_rest", [P, 1000])

        wout_hi = sb("wout_hi", [P, HC, DIM], F32R)
        wout_lo = sb("wout_lo", [P, HC, DIM], F32R)
        small_s = sb("small_s", [P, SMALL])
        ones_s = sb("ones_s", [1, P])
        rows_s = sb("rows_s", [P, ROWS, DIM])
        consts_s = sb("consts_s", [P, 2 * P + SCOLS + KC * EXPERTS])
        ident_s = consts_s[:, 0:P]
        maskq_f = consts_s[:, P:2 * P]
        maskk_f = consts_s[:, 2 * P:2 * P + SCOLS]
        gate_s = consts_s[:, 2 * P + SCOLS:].rearrange("p (k e) -> p k e", k=KC)
        maskq_s = sb("maskq_s", [P, P], BF16)
        maskk_s = sb("maskk_s", [P, SCOLS], BF16)
        ang = sb("ang", [P, 6, 32])
        table = sb("table", [P, 32])
        x5 = sb("x5", [P, STACKS, DIM])
        ropa = sb("ropa", [P, STACKS, DIM])
        ropb = sb("ropb", [P, STACKS, DIM])
        h = sb("h", [P, STACKS, DIM])
        xn = sb("xn", [P, STACKS, DIM])
        power = sb("power", [P, STACKS])
        ssq = sb("ssq", [P, STACKS])
        var = sb("var", [P, 4, STACKS])
        rstd = sb("rstd", [P, 4, STACKS])
        stats = sb("stats", [P, STACKS, 6])
        mv = sb("mv", [P, 3, STACKS, 2])
        xT_hi = sb("xT_hi", [P, KC, SLOTS], F32R)
        xT_lo = sb("xT_lo", [P, KC, SLOTS], F32R)
        hb = sb("hb", [P, STACKS, DIM])
        prob = sb("prob", [P, DEPTH, Q4 * 2, 32])
        probT = sb("probT", [P, DEPTH, Q4 * 2, 32])
        smax = sb("smax", [P, DEPTH, Q4 * 2])
        ssum = sb("ssum", [P, DEPTH, Q4 * 2])
        gate_hi = sb("gate_hi", [P, KC, EXPERTS], F32R)
        gate_lo = sb("gate_lo", [P, KC, EXPERTS], F32R)
        zeros = sb("zeros", [P, BANK], BF16)
        logit = sb("logit", [P, STACKS, EXPERTS])
        gmax = sb("gmax", [P, STACKS])
        gsum = sb("gsum", [P, STACKS])
        gprob = sb("gprob", [P, STACKS, 16])
        gtop = sb("gtop", [P, STACKS, 8])
        gfind = sb("gfind", [P, STACKS, 8])
        gleft = sb("gleft", [P, STACKS, 16])
        comb = sb("comb", [P, STACKS, EXPERTS])

        ps = ctx.enter_context(nc.psum_tensor("ps", [P, 8, BANK], F32))

        ld_x = [sem(f"ld_x{c}") for c in range(C_PARTS)]
        ld_small, ld_w2, ld_w3, ld_w45 = sem("ld_small"), sem("ld_w2"), sem("ld_w3"), sem("ld_w45")
        ld_rows, ld_consts = sem("ld_rows"), sem("ld_consts")
        ld_qkv = [sem(f"ld_qkv{i}") for i in range(6)]
        ld_raw = [sem(f"ld_raw{i}") for i in range(RAW_SLOTS)]
        pad_zero, end_zero = sem("pad_zero"), sem("end_zero")
        const_ready, prob_zero = sem("const_ready"), sem("prob_zero")
        conv1_mm, conv1_act = sem("conv1_mm"), sem("conv1_act")
        conv2_mm, conv2_act, conv2_up = sem("conv2_mm"), sem("conv2_act"), sem("conv2_up")
        conv3_mm, conv3_act = sem("conv3_mm"), sem("conv3_act")
        conv4_mm, conv4_act = sem("conv4_mm"), sem("conv4_act")
        conv5_mm, conv5_act = sem("conv5_mm"), sem("conv5_act")
        angle, sines, table_ready = sem("angle"), sem("sines"), sem("table_ready")
        gate_split, zeros_ready = sem("gate_split"), sem("zeros_ready")
        rope_part, rope_y = sem("rope_part"), sem("rope_y")
        squares, rstd_var = sem("squares"), sem("rstd_var")
        root = [sem(f"root{i}") for i in range(4)]
        stat_ready = [None] + [sem(f"stat_ready{i}") for i in range(1, 4)]
        mv_ready = [None] + [sem(f"mv_ready{i}") for i in range(1, 4)]
        h_ready = sem("h_ready")
        xn_ready, xT_mm, xT_high, xT_low = sem("xn_ready"), sem("xT_mm"), sem("xT_high"), sem("xT_low")
        raw_low_pool = sem("raw_low_pool")
        qkv_high, qkv_low, qkv_low_pool = sem("qkv_high"), sem("qkv_low"), sem("qkv_low_pool")
        proj_mm, proj_out = sem("proj_mm"), sem("proj_out")
        score_mm, s_max, s_shift, s_exp = sem("score_mm"), sem("s_max"), sem("s_shift"), sem("s_exp")
        s_sum, s_inv, s_norm, s_turn = sem("s_sum"), sem("s_inv"), sem("s_norm"), sem("s_turn")
        pv_mm, att_high, att_low, att_zero = sem("pv_mm"), sem("att_high"), sem("att_low"), sem("att_zero")
        out_mm, out_bias = sem("out_mm"), sem("out_bias")
        ln_scaled, hb_ready = sem("ln_scaled"), sem("hb_ready")
        raw_high, raw_low = sem("raw_high"), sem("raw_low")
        gate_mm, g_step, g_exp, comb_ready = sem("gate_mm"), sem("g_step"), sem("g_exp"), sem("comb_ready")
        up_mm, relu_done, sq_done = sem("up_mm"), sem("relu_done"), sem("sq_done")
        hid_high, hid_low = sem("hid_high"), sem("hid_low")
        down_mm, mixed = sem("down_mm"), sem("mixed")
        stored = sem("stored")

        def v(s, *halves):
            return ("project", [("v", s, half) for half in halves])

        def qk(p, first=0, end=4):
            return ("project", [(kind, hc) for hc in (2 * p, 2 * p + 1) for kind in "qk"][first:end])

        plan = [v(0, 0), ("turn 1", 1), v(0, 1), ("turn 1", 2), qk(0),
                ("scores", 0), qk(1),
                ("scores", 1), qk(2),
                ("scores", 2), qk(3, 0, 2), ("pv", 0), qk(3, 2, 4),
                ("scores", 3), v(1, 0), ("pv", 1), v(1, 1),
                ("scores", 4), v(2, 0), ("pv", 2), v(2, 1),
                ("scores", 5), ("pv", 3),
                ("scores", 6), ("pv", 4),
                ("scores", 7), ("out", 0),
                ("scores", 8), ("residual", 0), ("pv", 5),
                ("scores", 9), ("normalize", 0), ("pv", 6),
                ("scores", 10), ("pv", 7),
                ("scores", 11), ("pv", 8), ("finish", 11), ("out", 1), ("pv", 9), ("residual", 1), ("turn 2", 0),
                ("pv", 10), ("normalize", 1), ("pv", 11), ("turn 2", 1), ("out", 2)]
        items = [it for what, some in plan if what == "project" for it in some]
        item_at = {it: i for i, it in enumerate(items)}

        def done_before(kind, step):
            return sum(what == kind for what, _ in plan[:plan.index(step)])

        piece_order = [4, 5, 0, 2, 1, 3]
        DVE_LOW = 4

        def piece_of(it):
            if it[0] == "v":
                return 4 + it[2]
            return (0 if it[0] == "q" else 2) + it[1] // 4

        split_after = {u: [] for u in range(UNITS)}
        for n in range(PIECES * (1 + SPLIT_SLOTS)):
            split_after[n if n < PIECES else PIECES + 1 + (n - PIECES) * 7 // 12].append(divmod(n, PIECES))
        POOL_SPLITS = 3

        def low_split(j, pieces):
            if j == POOL_SPLITS:
                return raw_low_pool, pieces
            return raw_low, PIECES * (j if j < POOL_SPLITS else j - 1) + pieces

        def steps_of(u):
            at = plan.index(("scores", u))
            end = plan.index(("scores", u + 1)) if u + 1 < UNITS else len(plan)
            return plan[at + 1:end]

        def moving(x, kc, first=0, end=GROUPS):
            return x[:, kc, :].rearrange("p (g t) -> p g t", t=32)[:, first:end, 0:GT]

        def down_at(e, s):
            if e == EXPERTS - 1:
                return ps[:, (6, 7, 0)[s], 0:DIM]
            return ps[:, 4 + 2 * (e % 2) + s // 2, DIM * (s % 2):DIM * (s % 2) + DIM]

        def pads(x):
            g = x.rearrange("p n (g t) -> p n g t", t=32)
            return g[:, :, 0:GROUPS, GT:], g[:, :, GROUPS, :]

        def product(pe, dst, pairs):
            for i, ((w_hi, w_lo), (x_hi, x_lo)) in enumerate(pairs):
                pe.matmul(dst, w_hi, x_hi, start=(i == 0), stop=False)
                pe.matmul(dst, w_hi, x_lo, start=False, stop=False)
                last = pe.matmul(dst, w_lo, x_hi, start=False, stop=(i == len(pairs) - 1))
            return last

        def att_copy(dst, u):
            s, p, quads = unit_of(u)
            base = 0 if u < SHARED_PV else PROJ_BANK
            d = dst[:, 2 * p:2 * p + 2, P * s:P * (s + 1)].rearrange("p c (q i) -> p q c i", q=Q4)
            a = ps[:, base:base + Q4, 0:SCOLS].rearrange("p q (c t) -> p q c t", t=GT)
            return d[:, 0:quads, :, 0:GT], a[:, 0:quads]

        block = ctx.enter_context(nc.Block())

        @block.sync
        def _(sp):
            for c in range(C_PARTS):
                a = slice(P + BANK * c if c else 0, P + BANK * (c + 1))
                sp.dma_start(xw_s[:, a], xw[:, a]).then_inc(ld_x[c], 16)
                if c == 0:
                    sp.dma_start(small_s[:], small).then_inc(ld_small, 16)
            sp.dma_start(w2_s[:], w2).then_inc(ld_w2, 16)
            sp.dma_start(w3_s[:], w3).then_inc(ld_w3, 16)
            qkv_v = w_qkv.rearrange("(k p) n -> p k n", p=P)

            def load_qkv(some):
                for i in some:
                    a = slice(BANK * i, BANK * (i + 1))
                    sp.dma_start(qkv_raw[:, :, a], qkv_v[:, :, a]).then_inc(ld_qkv[i], 16)

            load_qkv(piece_order[0:2])
            sp.dma_start(w45_s[:], w45).then_inc(ld_w45, 16)
            sp.dma_start(rows_s[:].rearrange("p a b -> p (a b)"), rows.broadcast_to([P, ROWS * DIM])).then_inc(ld_rows, 16)
            load_qkv(piece_order[2:6])
            sp.dma_start(consts_s[:], consts).then_inc(ld_consts, 16)
            sp.wait_ge(conv5_mm, STACKS)
            for j in range(EXPERTS + 1):
                slot = j % RAW_SLOTS
                if j >= RAW_SLOTS:
                    sp.wait_ge(raw_high, PIECES * (j - RAW_SLOTS + 1))
                    sp.wait_ge(*low_split(j - RAW_SLOTS, PIECES))
                if j == 0:
                    sp.dma_start(raw[:, slot, :].rearrange("p (k d) -> p k d", k=HC),
                                 w_out.rearrange("(k p) d -> p k d", p=P)).then_inc(ld_raw[slot], 32)
                    continue
                e = j - 1
                sp.dma_start(raw[:, slot, 0:KC * HIDDEN].rearrange("p (k n) -> p k n", k=KC),
                             W1[e].rearrange("(k p) n -> p k n", p=P)).then_inc(ld_raw[slot], 16)
                sp.dma_start(raw[:, slot, KC * HIDDEN:].rearrange("p (k n) -> p k n", k=HK),
                             W2[e].rearrange("(k p) n -> p k n", p=P)).then_inc(ld_raw[slot], 16)
            out_rows = out.rearrange("b t d -> (b t) d")
            for g in range(GROUPS):
                s, q = divmod(g, Q4)
                sp.wait_ge(mixed, STACKS * (EXPERTS - 1) + s + 1)
                n = min(GT, CLIPS * FRAMES - GT * g)
                sp.dma_start(out_rows[GT * g:GT * g + n, :], h[32 * q:32 * q + n, s, :]).then_inc(stored, 16)
            sp.wait_ge(stored, 16 * GROUPS)

        @block.tensor
        def _(pe):
            def keep_warm(n, bank, columns=BANK):
                for _ in range(n):
                    pe.matmul(ps[:, bank, 0:columns], zeros[:, 0:P], zeros[:, 0:columns], start=True, stop=True)

            pe.wait_ge(zeros_ready, 1)
            keep_warm(WARM[0], 7)
            for c in range(C_PARTS):
                pe.wait_ge(ld_x[c], 16)
                pe.matmul(ps[:, c, :], xw_s[:, 0:P], xw_s[:, P + BANK * c:P + BANK * (c + 1)], start=True, stop=True)\
                  .then_inc(conv1_mm, 1)
            pe.wait_ge(ld_w2, 16)
            pe.wait_ge(pad_zero, 1)
            pe.wait_ge(end_zero, 1)
            for c in range(C_PARTS):
                pe.wait_ge(conv1_act, c + 1)
                for b in range(2):
                    at = (C1_STEP * c + b) * CLIPS
                    mm = pe.matmul(ps[0:C2, 3 + c, :], w2_s[:, b, :], h1[:, at:at + BANK], start=(b == 0), stop=(b == 1))
                mm.then_inc(conv2_mm, 1)
            keep_warm(WARM[1], 7)
            pe.wait_ge(ld_w3, 16)
            pe.wait_ge(pad_zero, 3)
            pe.wait_ge(conv2_act, C_PARTS)
            pe.wait_ge(conv2_up, C_PARTS)
            for m in range(KC):
                for j in range(PAIRS):
                    k = P if 2 * j + 1 < K3 else C2
                    x = h2[0:k, 2 * j:2 * j + S3 * (FRAMES - 1) + 1:S3, :]
                    mm = pe.matmul(ps[:, 6 + m, 0:FRAMES * CLIPS], w3_s[0:k, j, P * m:P * (m + 1)], x,
                                   start=(j == 0), stop=(j == PAIRS - 1))
                mm.then_inc(conv3_mm, 1)
            pe.wait_ge(ld_w45, 16)
            for m in range(KC):
                pe.wait_ge(conv3_act, m + 1)
                for j in range(3):
                    mm = pe.matmul(ps[:, m, 0:FRAMES * CLIPS], w4_s[:, m, j, :], h3[:, m, j:j + FRAMES, :],
                                   start=(j == 0), stop=(j == 2))
                mm.then_inc(conv4_mm, 1)
            pe.wait_ge(const_ready, 1)
            pe.wait_ge(ld_rows, 16)
            for s in range(STACKS):
                pe.matmul(ps[:, 2 + s, 0:DIM], ones_s[:], rows_s[0:1, ROW_B5, :], start=True, stop=False)
            pe.wait_ge(conv4_act, KC)
            for s in range(STACKS):
                for k in range(KC):
                    mm = pe.matmul(ps[:, 2 + s, 0:DIM], h4[:, k, P * s:P * (s + 1)], w5_s[:, k, :],
                                   start=False, stop=(k == KC - 1))
                mm.then_inc(conv5_mm, 1)

            def turn(n, s, bank):
                pe.wait_ge(xn_ready, STACKS * n + s + 1)
                for k in range(KC):
                    mm = pe.transpose(ps[:, bank, P * k:P * (k + 1)], xn[:, s, P * k:P * (k + 1)], ident_s)
                mm.then_inc(xT_mm, 1)

            def split_ready(n):
                pe.wait_ge(xT_high, n)
                pe.wait_ge(xT_low, n)

            def project(some):
                for it in some:
                    i = item_at[it]
                    piece = piece_order.index(piece_of(it)) + 1
                    pe.wait_ge(qkv_high, piece)
                    if piece <= DVE_LOW:
                        pe.wait_ge(qkv_low, piece)
                    else:
                        pe.wait_ge(qkv_low_pool, piece - DVE_LOW)
                    if i >= 4:
                        pe.wait_ge(proj_out, i - 3)
                    bank = PROJ_BANK + i % 4
                    if it[0] == "v":
                        _, s, half = it
                        at = 2 * INNER + half * BANK
                        mm = product(pe, ps[:, bank, :],
                                     [((xT_hi[:, k, P * s:P * (s + 1)], xT_lo[:, k, P * s:P * (s + 1)]),
                                       (qkv_hi[:, k, at:at + BANK], qkv_lo[:, k, at:at + BANK])) for k in range(KC)])
                    else:
                        at = (0 if it[0] == "q" else INNER) + it[1] * P
                        mm = product(pe, ps[:, bank, 0:TOK],
                                     [((qkv_hi[:, k, at:at + P], qkv_lo[:, k, at:at + P]),
                                       (moving(xT_hi, k), moving(xT_lo, k))) for k in range(KC)])
                    mm.then_inc(proj_mm, 1)

            def scores(u):
                s, p, quads = unit_of(u)
                if s == 0:
                    pe.wait_ge(proj_out, item_at[("k", 2 * p + 1)] + 1)
                if u >= 1:
                    pe.wait_ge(s_shift, u)
                shared = min(SHARED_PV, done_before("pv", ("scores", u)))
                if shared and u <= SHARED_PV + 2:
                    pe.wait_ge(att_high, shared)
                    pe.wait_ge(att_low, shared)
                for b in range(Q4):
                    pe.matmul(ps[:, b, 0:SCOLS], maskq_s[32 * b:32 * b + GROUP_CLIPS, :],
                              maskk_s[32 * b:32 * b + GROUP_CLIPS, :], start=True, stop=True)
                for hcl in range(2):
                    for q in range(quads):
                        g = Q4 * s + q
                        for b in range(Q4):
                            rows_ = slice(32 * b, 32 * b + 32)
                            mm = pe.matmul(ps[32 * q:32 * q + GT, b, GT * hcl:GT * (hcl + 1)],
                                           qT[rows_, 2 * p + hcl, GT * g:GT * (g + 1)],
                                           kT[rows_, 2 * p + hcl, GT * g:GT * (g + 1)],
                                           start=False, stop=True, skip_group_check=True)
                mm.then_inc(score_mm, 1)

            def pv(u):
                s, p, quads = unit_of(u)
                pe.wait_ge(s_turn, u + 1)
                if p == 0:
                    pe.wait_ge(proj_out, item_at[("v", s, 1)] + 1)
                if quads == Q4 and done_before("out", ("pv", u)):
                    pe.wait_ge(out_bias, done_before("out", ("pv", u)))
                if u < SHARED_PV:
                    pe.wait_ge(s_shift, done_before("scores", ("pv", u)))
                elif u == SHARED_PV:
                    pe.wait_ge(proj_out, len(items))
                else:
                    pe.wait_ge(att_high, u)
                    pe.wait_ge(att_low, u)
                base = 0 if u < SHARED_PV else PROJ_BANK
                for hcl in range(2):
                    for b in range(Q4):
                        head = 4 * (2 * p + hcl) + b
                        for q in range(quads):
                            mm = pe.matmul(ps[32 * b:32 * b + 32, base + q, GT * hcl:GT * (hcl + 1)],
                                           v_s[32 * q:32 * q + GT, s, 32 * head:32 * head + 32],
                                           probT[32 * q:32 * q + GT, u % DEPTH, 2 * b + hcl, 0:GT],
                                           start=True, stop=True)
                mm.then_inc(pv_mm, 1)

            def out_project(s):
                pe.wait_ge(att_high, PAIR_COUNT * (s + 1))
                pe.wait_ge(att_low, PAIR_COUNT * (s + 1))
                if s == 0:
                    pe.wait_ge(raw_high, PIECES)
                    pe.wait_ge(raw_low, PIECES)
                if s < STACKS - 1:
                    with_quad_3 = min(done_before("pv", ("out", s)), (GROUPS // Q4) * PAIR_COUNT)
                    pe.wait_ge(att_high, with_quad_3)
                    pe.wait_ge(att_low, with_quad_3)
                else:
                    pe.wait_ge(s_shift, UNITS)
                a = slice(P * s, P * (s + 1))
                product(pe, ps[:, OUT_BANK[s], 0:DIM],
                        [((att_hi[:, hc, a], att_lo[:, hc, a]), (wout_hi[:, hc, :], wout_lo[:, hc, :]))
                         for hc in range(HC)]).then_inc(out_mm, 1)

            pe.wait_ge(ld_consts, 16)
            keep_warm(WARM[2], 7)
            turn(0, 0, 0)
            keep_warm(WARM[3], 7)
            split_ready(1)
            for what, arg in plan:
                if what == "turn 1":
                    turn(0, arg, arg)
                elif what == "project":
                    if arg[0] == ("q", 0):
                        split_ready(STACKS)
                    if arg[0][0] == "v":
                        split_ready(arg[0][1] + 1)
                    project(arg)
                elif what == "scores":
                    if arg == 0:
                        pe.wait_ge(const_ready, 2)
                    scores(arg)
                elif what == "pv":
                    pv(arg)
                elif what == "turn 2":
                    if arg == 0:
                        pe.wait_ge(s_shift, UNITS)
                    turn(1, arg, TURN_BANK[arg])
                elif what == "out":
                    out_project(arg)

            def up(e, first=0, end=GROUPS):
                pe.wait_ge(raw_high, PIECES * (e + 1) + PIECES // 2)
                pe.wait_ge(*low_split(e + 1, PIECES // 2))
                slot = e % SPLIT_SLOTS
                for m in range(HK):
                    n = HK * e + m
                    if n >= 4 and first == 0:
                        pe.wait_ge(relu_done, n - 3)
                    if n == 3:
                        pe.wait_ge(out_bias, STACKS)
                    pairs = []
                    for k in range(KC):
                        at = k * HIDDEN + P * m
                        pairs.append(((exp_hi[:, slot, at:at + P], exp_lo[:, slot, at:at + P]),
                                      (moving(xT_hi, k, first, end), moving(xT_lo, k, first, end))))
                    mm = product(pe, ps[:, UP_BANK[n % 4], GT * first:GT * end], pairs)
                    if end == GROUPS:
                        mm.then_inc(up_mm, 1)

            def gate(s):
                a = slice(P * s, P * (s + 1))
                product(pe, ps[:, 6, EXPERTS * s:EXPERTS * (s + 1)],
                        [((xT_hi[:, k, a], xT_lo[:, k, a]), (gate_hi[:, k, :], gate_lo[:, k, :]))
                         for k in range(KC)]).then_inc(gate_mm, 1)

            def down(e):
                pe.wait_ge(hid_high, HK * (e + 1))
                pe.wait_ge(hid_low, HK * (e + 1))
                if e >= 2:
                    pe.wait_ge(mixed, STACKS * (e - 1))
                pe.wait_ge(raw_high, PIECES * (e + 2))
                pe.wait_ge(*low_split(e + 1, PIECES))
                slot = e % SPLIT_SLOTS
                for s in range(STACKS):
                    pairs = []
                    for k in range(HK):
                        at = KC * HIDDEN + k * DIM
                        n = HK * (e % 2) + k
                        pairs.append(((hid_hi[:, n, P * s:P * (s + 1)], hid_lo[:, n, P * s:P * (s + 1)]),
                                      (exp_hi[:, slot, at:at + DIM], exp_lo[:, slot, at:at + DIM])))
                    product(pe, down_at(e, s), pairs).then_inc(down_mm, 1)

            split_ready(STACKS + 2)
            up(0, 0, 2 * Q4)
            pe.wait_ge(gate_split, 2)
            gate(0)
            gate(1)
            keep_warm(WARM[4], 5)
            pe.wait_ge(out_bias, 2)
            turn(1, 2, TURN_BANK[2])
            keep_warm(WARM[5], 5)
            split_ready(STACKS + 3)
            up(0, 2 * Q4, GROUPS)
            gate(2)
            for e in range(EXPERTS):
                if e + 1 < EXPERTS:
                    up(e + 1)
                if e == 1:
                    pe.wait_ge(g_step, 1)
                down(e)

        @block.scalar
        def _(act):
            b1 = small_s[:, COL_B1:COL_B1 + 1]
            act.wait_ge(ld_small, 16)
            for c in range(C_PARTS):
                act.wait_ge(conv1_mm, c + 1)
                at, n = (C1_STEP * c + 1) * CLIPS, BANK
                if c == C_PARTS - 1:
                    n = BANK - CLIPS
                    act.activation(h1[0:64, at + n:at + BANK], ps[0:64, c, n:BANK], ACT.Gelu, bias=b1[0:64, :])
                act.activation(h1[:, at:at + n], ps[:, c, 0:n], ACT.Gelu, bias=b1).then_inc(conv1_act, 1)
            act.wait_ge(pad_zero, 2)
            for c in range(C_PARTS):
                act.wait_ge(conv2_mm, c + 1)
                at = PAD3 + C1_STEP * c
                act.activation(h2[0:C2, at:at + C1_STEP, :].rearrange("p a b -> p (a b)"), ps[0:C2, 3 + c, :], ACT.Gelu,
                               bias=small_s[0:C2, COL_B2:COL_B2 + 1]).then_inc(conv2_act, 1)
            act.wait_ge(angle, 8)
            act.activation(table[:], ang[:, 5, :], ACT.Sin).then_inc(sines, 1)
            for m in range(KC):
                act.wait_ge(conv3_mm, m + 1)
                act.activation(h3[:, m, 1:1 + FRAMES, :].rearrange("p a b -> p (a b)"), ps[:, 6 + m, 0:FRAMES * CLIPS],
                               ACT.Gelu, bias=small_s[:, COL_B3 + m:COL_B3 + m + 1]).then_inc(conv3_act, 1)
            act.wait_ge(pad_zero, 4)
            for m in range(KC):
                act.wait_ge(conv4_mm, m + 1)
                bias = small_s[:, COL_B4 + m:COL_B4 + m + 1]
                src = ps[:, m, 0:FRAMES * CLIPS].rearrange("p (t b) -> p b t", t=FRAMES)
                dst = h4[:, m, :].rearrange("p (g i) -> p g i", i=32)
                full = FULL_GROUPS * GROUP_CLIPS
                act.activation(dst[:, 0:FULL_GROUPS, 0:GT].rearrange("p g (b t) -> p g b t", t=FRAMES),
                               src[:, 0:full, :].rearrange("p (g b) t -> p g b t", b=GROUP_CLIPS), ACT.Gelu, bias=bias)
                act.activation(dst[:, FULL_GROUPS, 0:REST_CLIPS * FRAMES].rearrange("p (b t) -> p b t", t=FRAMES),
                               src[:, full:CLIPS, :], ACT.Gelu, bias=bias).then_inc(conv4_act, 1)
            for s in range(STACKS):
                act.wait_ge(conv5_mm, s + 1)
                act.activation(x5[:, s, :], ps[:, 2 + s, 0:DIM], ACT.Gelu).then_inc(conv5_act, 1)
            for s in range(STACKS):
                act.wait_ge(rope_y, s + 1)
                act.activation(xn[:, s, :], ropa[:, s, :], ACT.Square, accum_out=ssq[:, s:s + 1]).then_inc(squares, 1)

            def turned(n, s, bank):
                act.wait_ge(xT_mm, STACKS * n + s + 1)
                src = ps[:, bank, 0:KC * P].rearrange("p (k i) -> p k i", k=KC)
                act.activation(xT_hi[:, :, P * s:P * (s + 1)], src, ACT.Copy).then_inc(xT_high, 1)

            def copy_out(some):
                for it in some:
                    i = item_at[it]
                    act.wait_ge(proj_mm, i + 1)
                    bank = PROJ_BANK + i % 4
                    if it[0] == "v":
                        dst, src = v_s[:, it[1], BANK * it[2]:BANK * (it[2] + 1)], ps[:, bank, :]
                    else:
                        dst, src = (qT if it[0] == "q" else kT)[:, it[1], :], ps[:, bank, 0:TOK]
                    act.activation(dst, src, ACT.Copy).then_inc(proj_out, 1)

            def exponentials(u):
                act.wait_ge(s_shift, u + 1)
                e = prob[:, u % DEPTH, :, 0:GT]
                act.activation(e, e, ACT.Exp, scale=SCALE).then_inc(s_exp, 1)

            def attended(u):
                act.wait_ge(pv_mm, u + 1)
                if u == 0:
                    act.wait_ge(att_zero, 1)
                dst, src = att_copy(att_hi, u)
                act.activation(dst, src, ACT.Copy).then_inc(att_high, 1)

            def split(j, piece):
                act.wait_ge(ld_raw[j % RAW_SLOTS], 32 * (j // RAW_SLOTS + 1))
                if j >= 1:
                    if j <= SPLIT_SLOTS:
                        act.wait_ge(proj_mm, len(items))
                    else:
                        act.wait_ge(down_mm, STACKS * (j - SPLIT_SLOTS))
                a = slice(PIECE * piece, PIECE * (piece + 1))
                dst = wout_hi[:].rearrange("p k d -> p (k d)") if j == 0 else exp_hi[:, (j - 1) % SPLIT_SLOTS, :]
                act.activation(dst[:, a], raw[:, j % RAW_SLOTS, a], ACT.Copy).then_inc(raw_high, 1)

            def follow(steps):
                for what, arg in steps:
                    if what == "project":
                        copy_out(arg)
                    elif what == "turn 1":
                        turned(0, arg, arg)
                    elif what == "pv":
                        attended(arg)
                    elif what == "turn 2":
                        turned(1, arg, TURN_BANK[arg])

            turned(0, 0, 0)
            follow(plan[:plan.index(("scores", 0))])
            for u in range(UNITS):
                exponentials(u)
                follow(steps_of(u))
                for j, piece in split_after[u]:
                    split(j, piece)
            turned(1, 2, TURN_BANK[2])

            for e in range(EXPERTS):
                for m in range(HK):
                    n = HK * e + m
                    act.wait_ge(up_mm, n + 1)
                    if n >= 2:
                        act.wait_ge(sq_done, n - 1)
                        act.wait_ge(hid_high, n - 1)
                    act.activation(relu[:, n % 2, :], ps[:, UP_BANK[n % 4], 0:TOK], ACT.Relu).then_inc(relu_done, 1)
                    act.wait_ge(relu_done, n + 1)
                    if e >= 2:
                        act.wait_ge(down_mm, STACKS * (e - 1))
                    if n == 0:
                        act.wait_ge(pad_zero, 5)
                    dst = hid_hi[:, n % (2 * HK), :].rearrange("p (g t) -> p g t", t=32)[:, 0:GROUPS, 0:GT]
                    act.activation(dst, relu[:, n % 2, :].rearrange("p (g t) -> p g t", t=GT), ACT.Square)\
                       .then_inc(hid_high, 1)
                if e == 0:
                    act.wait_ge(g_step, 3)
                    act.activation(logit[:], logit[:], ACT.Exp).then_inc(g_exp, 1)
                if e >= 1 and e + 3 <= EXPERTS:
                    for piece in range(PIECES):
                        split(e + 3, piece)

        @block.gpsimd
        def _(pool):
            pool.memset(h1[:, 0:CLIPS], 0.0).then_inc(pad_zero, 1)
            pool.memset(h2[:, 0:PAD3, :], 0.0)
            pool.memset(h2[:, PAD3 + L2 - 1:, :], 0.0).then_inc(pad_zero, 1)
            pool.memset(h3[:, :, 0:FRAMES + 2:FRAMES + 1, :], 0.0).then_inc(pad_zero, 1)
            pool.memset(h4[:], 0.0).then_inc(pad_zero, 1)
            pool.memset(ones_s[:], 1.0).then_inc(const_ready, 1)
            pool.memset(power[:], -0.5)
            pool.memset(gprob[:], -1.0)
            pool.memset(gfind[:], -1.0)
            pool.memset(prob[:], 0.0).then_inc(prob_zero, 1)
            for n, i in list(enumerate(piece_order))[DVE_LOW:]:
                a = slice(BANK * i, BANK * (i + 1))
                pool.wait_ge(qkv_high, n + 1)
                pool.tensor_tensor(qkv_lo[:, :, a], qkv_raw[:, :, a], qkv_hi[:, :, a].bitcast(F32), ALU.subtract)\
                    .then_inc(qkv_low_pool, 1)

            n_root = [0]

            def inverse_root(kind, s, src, scale, eps):
                pool.tensor_scalar(var[:, kind, s:s + 1], src, scale, eps, ALU.mult, ALU.add).then_inc(rstd_var, 1)
                n_root[0] += 1
                pool.wait_ge(rstd_var, n_root[0])
                pool.tensor_tensor(rstd[:, kind, s:s + 1], var[:, kind, s:s + 1], power[:, 0:1], ALU.pow)\
                    .then_inc(root[kind], 1)

            def rms_root(s):
                pool.wait_ge(squares, s + 1)
                inverse_root(0, s, ssq[:, s:s + 1], 1.0 / DIM, RMS_EPS)

            def ln_root(kind, s):
                pool.wait_ge(mv_ready[kind], s + 1)
                inverse_root(kind, s, mv[:, kind - 1, s, 1:2], 1.0, ATT_EPS if kind == 2 else LN_EPS)

            rms_root(0)
            ln_root(1, 0)
            rms_root(1)
            ln_root(1, 1)
            rms_root(2)
            ln_root(1, 2)
            pool.wait_ge(ld_consts, 16)
            pool.tensor_copy(maskq_s[:], maskq_f)
            pool.tensor_copy(maskk_s[:], maskk_f).then_inc(const_ready, 1)
            pool.wait_ge(qkv_low, DVE_LOW)
            pool.wait_ge(qkv_low_pool, len(piece_order) - DVE_LOW)
            for x in (att_hi, att_lo):
                for pad in pads(x[:].bitcast(F32)):
                    ms = pool.memset(pad, 0.0)
            ms.then_inc(att_zero, 1)
            for s in range(STACKS):
                pool.tensor_tensor(hb[:, s, :], h[:, s, :], rows_s[:, ROW_BETA, :], ALU.add).then_inc(hb_ready, 1)

            def normed(u):
                pool.wait_ge(s_inv, u + 1)
                e = prob[:, u % DEPTH, :, 0:GT]
                pool.tensor_tensor(e, e, ssum[:, u % DEPTH, :, None].broadcast_to([P, Q4 * 2, GT]), ALU.mult)\
                    .then_inc(s_norm, 1)

            def split(piece):
                a = slice(PIECE * piece, PIECE * (piece + 1))
                slot = (POOL_SPLITS - 1) % SPLIT_SLOTS
                pool.wait_ge(raw_high, PIECES * POOL_SPLITS + piece + 1)
                pool.tensor_tensor(exp_lo[:, slot, a], raw[:, POOL_SPLITS % RAW_SLOTS, a],
                                   exp_hi[:, slot, a].bitcast(F32), ALU.subtract).then_inc(raw_low_pool, 1)

            for u in range(UNITS):
                if u:
                    normed(u - 1)
                for what, arg in steps_of(u):
                    if what == "out" and arg < STACKS - 1:
                        ln_root(2, arg)
                    elif what == "residual":
                        ln_root(3, arg)
                    elif what == "finish":
                        normed(arg)
                for j, piece in split_after[u]:
                    if j == POOL_SPLITS and u < UNITS - 1:
                        split(piece)
            pool.wait_ge(pv_mm, UNITS)
            for x in (hid_hi, hid_lo):
                for pad in pads(x[:].bitcast(F32)):
                    ms = pool.memset(pad, 0.0)
            ms.then_inc(pad_zero, 1)
            for j, piece in split_after[UNITS - 1]:
                if j == POOL_SPLITS:
                    split(piece)
            ln_root(2, 2)
            ln_root(3, 2)
            for n in range(HK * EXPERTS):
                pool.wait_ge(relu_done, n + 1)
                if n >= 2:
                    pool.wait_ge(hid_low, n - 1)
                pool.tensor_tensor(sq[:, n % 2, :], relu[:, n % 2, :], relu[:, n % 2, :], ALU.mult).then_inc(sq_done, 1)

        @block.vector
        def _(dve):
            dve.memset(zeros[:], 0.0).then_inc(zeros_ready, 1)
            dve.memset(h1[64:P, BLOCKS * CLIPS:], 0.0).then_inc(end_zero, 1)
            dve.wait_ge(ld_small, 16)
            phase = small_s[:, COL_PHASE:COL_PHASE + 32]
            n_angle = [0]

            def angle_step(ins):
                n_angle[0] += 1
                ins.then_inc(angle, 1)
                dve.wait_ge(angle, n_angle[0])

            angle_step(dve.tensor_scalar(ang[:, 0, :], small_s[:, COL_FREQ:COL_FREQ + 32], small_s[:, COL_FRAME:COL_FRAME + 1], None, ALU.mult))
            angle_step(dve.tensor_tensor(ang[:, 1, :], ang[:, 0, :], phase, ALU.add))
            angle_step(dve.tensor_scalar(ang[:, 2, :], ang[:, 1, :], 1.0 / (2 * PI), ROUNDER, ALU.mult, ALU.add))
            angle_step(dve.tensor_scalar(ang[:, 2, :], ang[:, 2, :], ROUNDER, None, ALU.subtract))
            angle_step(dve.scalar_tensor_tensor(out=ang[:, 3, :], in0=ang[:, 2, :], scalar=-TWO_PI_HI, in1=ang[:, 0, :],
                                                op0=ALU.mult, op1=ALU.add))
            angle_step(dve.scalar_tensor_tensor(out=ang[:, 4, :], in0=ang[:, 2, :], scalar=-TWO_PI_MID, in1=ang[:, 3, :],
                                                op0=ALU.mult, op1=ALU.add))
            angle_step(dve.tensor_tensor(ang[:, 3, :], ang[:, 4, :], phase, ALU.add))
            angle_step(dve.tensor_scalar(ang[:, 5, :], ang[:, 3, :], 3.1415925, -3.1415925, ALU.min, ALU.max))

            def round_qkv(n):
                a = slice(BANK * piece_order[n], BANK * (piece_order[n] + 1))
                dve.wait_ge(ld_qkv[piece_order[n]], 16)
                dve.tensor_copy(qkv_hi[:, :, a], qkv_raw[:, :, a]).then_inc(qkv_high, 1)

            def rest_qkv(n):
                a = slice(BANK * piece_order[n], BANK * (piece_order[n] + 1))
                dve.wait_ge(qkv_high, n + 1)
                dve.tensor_tensor(qkv_lo[:, :, a], qkv_raw[:, :, a], qkv_hi[:, :, a].bitcast(F32), ALU.subtract)\
                   .then_inc(qkv_low, 1)

            def up_half(c):
                dve.wait_ge(conv2_act, c + 1)
                at = PAD3 + C1_STEP * c
                dve.tensor_copy(h2[C2:P, at - 1:at - 1 + C1_STEP, :], h2[0:C2, at:at + C1_STEP, :]).then_inc(conv2_up, 1)

            dve.wait_ge(pad_zero, 2)
            round_qkv(0)
            up_half(0)
            rest_qkv(0)
            up_half(1)
            round_qkv(1)
            up_half(2)
            rest_qkv(1)
            for n in (2, 3):
                round_qkv(n)
                rest_qkv(n)
            dve.wait_ge(sines, 1)
            dve.tensor_tensor(table[:], table[:], small_s[:, COL_SIGN:COL_SIGN + 32], ALU.mult).then_inc(table_ready, 1)
            for n in (4, 5):
                round_qkv(n)

            cos_b, sin_b = (table[:, None, i:i + 16].broadcast_to([P, 16, 16]) for i in (0, 16))
            dve.wait_ge(table_ready, 1)

            def rope_products(s):
                dve.wait_ge(conv5_act, s + 1)
                x, a, b = (t[:, s, :].rearrange("p (h d) -> p h d", d=16) for t in (x5, ropa, ropb))
                dve.tensor_tensor(a, x, cos_b, ALU.mult).then_inc(rope_part, 1)
                for i in range(2):
                    dve.tensor_tensor(b[:, :, i::2], x[:, :, 1 - i::2], sin_b[:, :, i::2], ALU.mult).then_inc(rope_part, 1)

            def rope_sum(s):
                dve.wait_ge(rope_part, 3 * (s + 1))
                dve.tensor_tensor(ropa[:, s, :], ropa[:, s, :], ropb[:, s, :], ALU.add).then_inc(rope_y, 1)

            def rms(s):
                dve.wait_ge(rope_y, s + 1)
                dve.wait_ge(root[0], s + 1)
                dve.scalar_tensor_tensor(out=h[:, s, :], in0=ropa[:, s, :], scalar=rstd[:, 0, s:s + 1],
                                         in1=rows_s[:, ROW_NORM, :], op0=ALU.mult, op1=ALU.mult).then_inc(h_ready, 1)

            def moments(kind, s, src, ready, count):
                dve.wait_ge(ready, count)
                dve.bn_stats(stats[:, s, :], src[:, s, :]).then_inc(stat_ready[kind], 1)
                dve.wait_ge(stat_ready[kind], s + 1)
                dve.bn_aggr(mv[:, kind - 1, s, :], stats[:, s, :]).then_inc(mv_ready[kind], 1)

            def normalize(kind, s):
                dve.wait_ge(root[kind], s + 1)
                dve.wait_ge(mv_ready[kind], s + 1)
                dve.tensor_scalar(xn[:, s, :], h[:, s, :], mv[:, kind - 1, s, 0:1], rstd[:, kind, s:s + 1],
                                  ALU.subtract, ALU.mult).then_inc(xn_ready, 1)

            def turned(n, s, bank):
                dve.wait_ge(xT_high, STACKS * n + s + 1)
                a = slice(P * s, P * (s + 1))
                src = ps[:, bank, 0:KC * P].rearrange("p (k i) -> p k i", k=KC)
                dve.tensor_tensor(xT_lo[:, :, a], src, xT_hi[:, :, a].bitcast(F32), ALU.subtract).then_inc(xT_low, 1)

            dve.wait_ge(ld_rows, 16)
            for s in (0, 1):
                rope_products(s)
                rope_sum(s)
            rms(0)
            moments(1, 0, h, h_ready, 1)
            rope_products(2)
            rope_sum(2)
            rms(1)
            normalize(1, 0)
            moments(1, 1, h, h_ready, 2)
            rms(2)
            turned(0, 0, 0)
            moments(1, 2, h, h_ready, 3)
            normalize(1, 1)
            normalize(1, 2)
            turned(0, 1, 1)
            turned(0, 2, 2)
            dve.tensor_copy(gate_hi[:], gate_s).then_inc(gate_split, 1)
            dve.wait_ge(gate_split, 1)
            dve.tensor_tensor(gate_lo[:], gate_s, gate_hi[:].bitcast(F32), ALU.subtract).then_inc(gate_split, 1)

            def top(u):
                dve.wait_ge(score_mm, u + 1)
                src = ps[:, 0:Q4, 0:SCOLS].rearrange("p b (c t) -> p b c t", t=GT)
                dve.tensor_reduce(smax[:, u % DEPTH].rearrange("p (b c) -> p b c", b=Q4), src, AX.X, ALU.max).then_inc(s_max, 1)

            def shift(u):
                dve.wait_ge(s_max, u + 1)
                if u == 0:
                    dve.wait_ge(prob_zero, 1)
                if u >= DEPTH:
                    dve.wait_ge(s_turn, u - DEPTH + 1)
                src = ps[:, 0:Q4, 0:SCOLS].rearrange("p b (c t) -> p b c t", t=GT)
                m = smax[:, u % DEPTH].rearrange("p (b c) -> p b c", b=Q4)
                dst = prob[:, u % DEPTH].rearrange("p (b c) t -> p b c t", b=Q4)[:, :, :, 0:GT]
                dve.tensor_tensor(dst, src, m[:, :, :, None].broadcast_to([P, Q4, 2, GT]), ALU.subtract).then_inc(s_shift, 1)

            def sums(u):
                dve.wait_ge(s_exp, u + 1)
                dve.tensor_reduce(ssum[:, u % DEPTH], prob[:, u % DEPTH, :, 0:GT], AX.X, ALU.add).then_inc(s_sum, 1)

            def inverse(u):
                dve.wait_ge(s_sum, u + 1)
                dve.reciprocal(ssum[:, u % DEPTH], ssum[:, u % DEPTH]).then_inc(s_inv, 1)

            def turn_probs(u):
                dve.wait_ge(s_norm, u + 1)
                if u >= DEPTH:
                    dve.wait_ge(pv_mm, u - DEPTH + 1)
                dve.transpose(probT[:, u % DEPTH].rearrange("p c t -> p (c t)"),
                              prob[:, u % DEPTH].rearrange("p c t -> p (c t)")).then_inc(s_turn, 1)

            def attended(u):
                dve.wait_ge(att_high, u + 1)
                (dst, src), (hi, _) = att_copy(att_lo, u), att_copy(att_hi, u)
                dve.tensor_tensor(dst, src, hi.bitcast(F32), ALU.subtract).then_inc(att_low, 1)

            def split(j, piece):
                dve.wait_ge(raw_high, PIECES * j + piece + 1)
                a = slice(PIECE * piece, PIECE * (piece + 1))
                if j == 0:
                    dst, hi = wout_lo[:].rearrange("p k d -> p (k d)"), wout_hi[:].rearrange("p k d -> p (k d)")
                else:
                    dst, hi = exp_lo[:, (j - 1) % SPLIT_SLOTS, :], exp_hi[:, (j - 1) % SPLIT_SLOTS, :]
                dve.tensor_tensor(dst[:, a], raw[:, j % RAW_SLOTS, a], hi[:, a].bitcast(F32), ALU.subtract)\
                   .then_inc(raw_low, 1)

            def biased(s):
                dve.wait_ge(out_mm, s + 1)
                dve.tensor_tensor(x5[:, s, :], ps[:, OUT_BANK[s], 0:DIM], rows_s[:, ROW_BOUT, :], ALU.add)\
                   .then_inc(out_bias, 1)
                moments(2, s, x5, out_bias, s + 1)

            def residual(s):
                dve.wait_ge(mv_ready[2], s + 1)
                dve.scalar_tensor_tensor(out=ropa[:, s, :], in0=x5[:, s, :], scalar=mv[:, 1, s, 0:1],
                                         in1=rows_s[:, ROW_GAMMA, :], op0=ALU.subtract, op1=ALU.mult).then_inc(ln_scaled, 1)
                dve.wait_ge(ln_scaled, s + 1)
                dve.wait_ge(root[2], s + 1)
                dve.wait_ge(hb_ready, s + 1)
                dve.scalar_tensor_tensor(out=h[:, s, :], in0=ropa[:, s, :], scalar=rstd[:, 2, s:s + 1],
                                         in1=hb[:, s, :], op0=ALU.mult, op1=ALU.add).then_inc(h_ready, 1)
                moments(3, s, h, h_ready, STACKS + s + 1)

            for u in range(UNITS):
                top(u)
                if u >= 1:
                    sums(u - 1)
                shift(u)
                if u >= 1:
                    inverse(u - 1)
                if u >= 1:
                    turn_probs(u - 1)
                for what, arg in steps_of(u):
                    if what == "pv":
                        attended(arg)
                    elif what == "out" and arg < STACKS - 1:
                        biased(arg)
                    elif what == "residual":
                        residual(arg)
                    elif what == "normalize":
                        normalize(3, arg)
                    elif what == "turn 2":
                        turned(1, arg, TURN_BANK[arg])
                    elif what == "finish":
                        sums(arg)
                        inverse(arg)
                        turn_probs(arg)
                for j, piece in split_after[u]:
                    if j != POOL_SPLITS:
                        split(j, piece)
            biased(2)
            residual(2)
            normalize(3, 2)
            turned(1, 2, TURN_BANK[2])

            def gate():
                n_gate = [0]

                def step(ins):
                    n_gate[0] += 1
                    ins.then_inc(g_step, 1)
                    dve.wait_ge(g_step, n_gate[0])

                def wide(x):
                    return x[:, :, None].broadcast_to([P, STACKS, EXPERTS])

                dve.wait_ge(gate_mm, STACKS)
                step(dve.tensor_copy(logit[:].rearrange("p s e -> p (s e)"), ps[:, 6, 0:STACKS * EXPERTS]))
                step(dve.tensor_reduce(gmax[:], logit[:], AX.X, ALU.max))
                step(dve.tensor_tensor(logit[:], logit[:], wide(gmax), ALU.subtract))
                dve.wait_ge(g_exp, 1)
                step(dve.tensor_reduce(gsum[:], logit[:], AX.X, ALU.add))
                step(dve.reciprocal(gsum[:], gsum[:]))
                probs = gprob[:, :, 0:EXPERTS]
                step(dve.tensor_tensor(probs, logit[:], wide(gsum), ALU.mult))
                for s in range(STACKS):
                    step(dve.max(gtop[:, s, :], gprob[:, s, 0:EXPERTS]))
                step(dve.tensor_copy(gfind[:, :, 0:2], gtop[:, :, 0:2]))
                for s in range(STACKS):
                    step(dve.match_replace(gleft[:, s, :], gfind[:, s, :], gprob[:, s, :], -2.0))
                step(dve.tensor_tensor(comb[:], gleft[:, :, 0:EXPERTS], probs, ALU.not_equal))
                step(dve.tensor_tensor(comb[:], comb[:], probs, ALU.mult))
                step(dve.tensor_tensor(gsum[:], gtop[:, :, 0], gtop[:, :, 1], ALU.add))
                step(dve.tensor_scalar(gsum[:], gsum[:], TOP_EPS, None, ALU.add))
                step(dve.reciprocal(gsum[:], gsum[:]))
                dve.tensor_tensor(comb[:], comb[:], wide(gsum), ALU.mult).then_inc(comb_ready, 1)

            def low_parts(e):
                for m in range(HK):
                    n = HK * e + m
                    dve.wait_ge(sq_done, n + 1)
                    dve.wait_ge(hid_high, n + 1)
                    if n == 0:
                        dve.wait_ge(pad_zero, 5)
                    hi, lo = (x[:, n % (2 * HK), :].rearrange("p (g t) -> p g t", t=32)[:, 0:GROUPS, 0:GT]
                              for x in (hid_hi, hid_lo))
                    dve.tensor_tensor(lo, sq[:, n % 2, :].rearrange("p (g t) -> p g t", t=GT), hi.bitcast(F32),
                                      ALU.subtract).then_inc(hid_low, 1)

            def mix(e):
                for s in range(STACKS):
                    dve.wait_ge(down_mm, STACKS * e + (s if e == EXPERTS - 1 else max(s, 1)) + 1)
                    if e:
                        dve.wait_ge(mixed, STACKS * (e - 1) + s + 1)
                    dve.scalar_tensor_tensor(out=h[:, s, :], in0=down_at(e, s), scalar=comb[:, s, e:e + 1], in1=h[:, s, :],
                                             op0=ALU.mult, op1=ALU.add).then_inc(mixed, 1)

            low_parts(0)
            gate()
            dve.wait_ge(comb_ready, 1)
            for e in range(EXPERTS):
                if e + 1 < EXPERTS:
                    low_parts(e + 1)
                mix(e)
                if e + 4 <= EXPERTS:
                    for piece in range(PIECES):
                        split(e + 4, piece)


_OUT = ((CLIPS, FRAMES, DIM), "float32")


def kernel(**inputs):
    import numpy as np
    import concourse.bacc as bacc
    from concourse.bass_utils import run_bass_kernel_spmd

    a = {k: np.ascontiguousarray(v) for k, v in inputs.items()}
    f = np.float32
    arrays = {}
    x = a["x"][:, 0, :]
    padded = np.zeros((CLIPS, PER * S1 * (BLOCKS - 1) + WINDOW + PAD1), f)
    padded[:, PAD1:PAD1 + x.shape[1]] = x
    windows = np.stack([padded[:, PER * S1 * w:PER * S1 * w + WINDOW].T for w in range(BLOCKS)], 1)
    w = np.zeros((WINDOW, PER, C1), f)
    for i in range(PER):
        w[S1 * i:S1 * i + K1, i, :] = a["L0_tok_w1"][:, 0, :].T
    arrays["xw"] = np.concatenate([w.reshape(WINDOW, P), windows.reshape(WINDOW, BLOCKS * CLIPS)], 1)
    slot = np.arange(P)
    small = np.zeros((P, SMALL), f)
    small[:, COL_FRAME] = slot % 32 % FRAMES
    small[:, COL_PHASE:COL_PHASE + 16] = PI / 2
    small[:, COL_SIGN:COL_SIGN + 32] = np.concatenate([np.ones(16, f), np.tile(np.array([-1.0, 1.0], f), 8)])
    mask_q, mask_k = np.zeros((P, P), f), np.zeros((P, SCOLS), f)
    for b in range(Q4):
        for c in range(GROUP_CLIPS):
            mask_q[32 * b + c] = (slot % 32 < GT) & (slot % 32 // FRAMES == c)
            mask_k[32 * b + c] = np.where(np.arange(SCOLS) % GT // FRAMES == c, 0.0, -2.0 ** 100)
    small[:, COL_B1] = np.tile(a["L0_tok_b1"], PER)
    small[:C2, COL_B2] = a["L0_tok_b2"]
    small[:, COL_B3:COL_B3 + 2] = a["L0_tok_b3"].reshape(KC, P).T
    small[:, COL_B4:COL_B4 + 2] = a["L0_tok_b4"].reshape(KC, P).T
    small[:, COL_FREQ:COL_FREQ + 32] = np.tile(np.repeat(a["L0_tok_rope_freqs"], 2), 2)
    arrays["small"] = small
    w = np.zeros((2, PER, C1, C2), f)
    for j in range(K2):
        at = PER - PAD2 + j
        w[at // PER, at % PER] = a["L0_tok_w2"][:, :, j].T
    arrays["w2"] = w.reshape(2, P, C2).transpose(1, 0, 2)
    w = np.zeros((2 * PAIRS, C2, C3), f)
    w[:K3] = a["L0_tok_w3"].transpose(2, 1, 0)
    arrays["w3"] = w.reshape(PAIRS, P, C3).transpose(1, 0, 2)
    w = np.zeros((P, KC, 3, P), f)
    per_group = a["L0_tok_w4"].shape[1]
    for o in range(DIM):
        first = o % P // per_group * per_group
        w[first:first + per_group, o // P, :, o % P] = a["L0_tok_w4"][o]
    w5 = a["L0_tok_w5"][:, :, 0].T.reshape(KC, P, DIM).transpose(1, 0, 2)
    arrays["w45"] = np.concatenate([w.reshape(P, -1), w5.reshape(P, -1)], 1)
    arrays["rows"] = np.concatenate([a[k] for k in ("L0_tok_norm_w", "L0_attn_b_out", "L0_attn_ln_gamma",
                                                    "L0_attn_ln_beta", "L0_tok_b5")]).reshape(1, ROWS * DIM)
    gate = a["L0_ffn_Wg"].reshape(KC, P, EXPERTS).transpose(1, 0, 2).reshape(P, -1)
    arrays["consts"] = np.concatenate([np.eye(P, dtype=f), mask_q, mask_k, gate], 1)
    arrays["w_qkv"] = a["L0_attn_w_qkv"]
    arrays["w_out"] = a["L0_attn_w_out"]
    arrays["W1"] = a["L0_ffn_W1"]
    arrays["W2"] = a["L0_ffn_W2"]

    nc = bacc.Bacc("TRN2", target_bir_lowering=False, num_devices=1)
    sent, args = {}, []
    for name, value in arrays.items():
        sent[f"in_{name}"] = np.ascontiguousarray(value)
        args.append(nc.dram_tensor(f"in_{name}", value.shape, mybir.dt.from_np(value.dtype), kind="ExternalInput").ap())
    out = nc.dram_tensor("out_tokens", _OUT[0], mybir.dt.from_np(np.dtype(_OUT[1])), kind="ExternalOutput").ap()
    build(nc, *args, out)
    return run_bass_kernel_spmd(nc, [sent], core_ids=[0]).results[0]["out_tokens"]
```

```python
from contextlib import ExitStack

import concourse.bass as bass
from concourse import mybir

F32 = mybir.dt.float32
F32R = mybir.dt.float32r
BF16 = mybir.dt.bfloat16
ALU = mybir.AluOpType
ACT = mybir.ActivationFunctionType
AX = mybir.AxisListType

P = 128
CLIPS = 64
FRAMES = 5
DIM = 256
KC = DIM // P
HEADS, HEAD_DIM = 32, 32
INNER = HEADS * HEAD_DIM
HC = INNER // P
EXPERTS, HIDDEN = 8, 512
HK = HIDDEN // P
Q4 = 4

GROUP_CLIPS = 6
GT = GROUP_CLIPS * FRAMES
GROUPS = -(-CLIPS // GROUP_CLIPS)
STACKS = -(-GROUPS // Q4)
SLOTS = STACKS * P
TOK = GROUPS * GT
FULL_GROUPS = CLIPS // GROUP_CLIPS
REST_CLIPS = CLIPS - FULL_GROUPS * GROUP_CLIPS

C1, K1, S1, PAD1 = 32, 15, 8, 7
PER = 4
WINDOW = S1 * (PER - 1) + K1
L1 = 94
BLOCKS = 24
C2, K2, PAD2 = 64, 7, 3
L2 = 24
C3, K3, S3, PAD3 = 256, 9, 5, 4
PAIRS = (K3 + 1) // 2
H2_COLS = (PAD3 + L2) // 2 + 1
PARITIES = 2
BANK = 512
C1_STEP = BANK // CLIPS
C_PARTS = BLOCKS // C1_STEP

PAIR_COUNT = HC // 2
UNITS = STACKS * PAIR_COUNT
DEPTH = 3
SCOLS = 2 * GT
PROJ_BANK = 4
SHARED_PV = 3
OUT_BANK = (7, 3, 0)
TURN_BANK = (7, 7, 7)
UP_BANK = (1, 2, 3, 0)
WARM = (5, 3, 20, 4, 3, 5)
POOL_STORES = (1, 3, 5)
RAW_SLOTS, SPLIT_SLOTS = 4, 3
ECOLS = KC * HIDDEN + HK * DIM
PIECES = 4
PIECE = ECOLS // PIECES

SCALE = float(HEAD_DIM) ** -0.5
PI = 3.14159265358979
TWO_PI_HI, TWO_PI_MID, TWO_PI_LO = 6.28125, 1.9353071693331003e-03, 1.025271e-11
ROUNDER = 12582912.0
LN_EPS, RMS_EPS, ATT_EPS, TOP_EPS = 1e-5, 1e-8, 1e-6, 1e-8

COL_B1, COL_B2, COL_B3, COL_B4, COL_FRAME, COL_FREQ, COL_PHASE, COL_SIGN, SMALL = 0, 1, 2, 4, 6, 7, 39, 71, 103
ROW_NORM, ROW_BOUT, ROW_GAMMA, ROW_BETA, ROW_B5, ROWS = range(6)


def unit_of(u):
    s, p = divmod(u, PAIR_COUNT)
    return s, p, min(Q4, GROUPS - Q4 * s)


def pv_bank(u):
    return 0 if u < SHARED_PV or u == UNITS - 2 else PROJ_BANK


def build(nc, xw, small, w2, w3, w45, rows, consts, w_qkv, w_out, W1, W2, out):
    with ExitStack() as ctx:
        def sb(name, shape, dt=F32, life=ctx):
            return life.enter_context(nc.sbuf_tensor(name, shape, dt))

        def sem(name):
            return ctx.enter_context(nc.semaphore(name))

        with ExitStack() as conv:
            xw_s = sb("xw_s", [WINDOW, P + BLOCKS * CLIPS], life=conv)
            w2_s = sb("w2_s", [P, 3, P], life=conv)
            w3_s = sb("w3_s", [P, PARITIES, PAIRS, C3], life=conv)
            w45_s = sb("w45_s", [P, KC * 3 * P + KC * DIM], life=conv)
            h1 = sb("h1", [P, (BLOCKS + 1) * CLIPS], life=conv)
            h2 = sb("h2", [P, H2_COLS, CLIPS], life=conv)
            h3 = sb("h3", [P, KC, FRAMES + 2, CLIPS], life=conv)
            h4 = sb("h4", [P, KC, SLOTS], life=conv)
        raw = sb("raw", [P, RAW_SLOTS, ECOLS])
        w4_s = w45_s[:, 0:KC * 3 * P].rearrange("p (m j o) -> p m j o", m=KC, j=3)
        w5_s = w45_s[:, KC * 3 * P:].rearrange("p (k o) -> p k o", k=KC)
        sb("conv_rest", [P, 1920])
        with ExitStack() as early:
            qkv_raw = sb("qkv_raw", [P, KC, 3 * INNER], life=early)
        att_hi = sb("att_hi", [P, HC, SLOTS], F32R)
        att_lo = sb("att_lo", [P, HC, SLOTS], F32R)
        with ExitStack() as early:
            qkv_hi = sb("qkv_hi", [P, KC, 3 * INNER], F32R, life=early)
            qkv_lo = sb("qkv_lo", [P, KC, 3 * INNER], F32R, life=early)
        exp_hi = sb("exp_hi", [P, SPLIT_SLOTS, ECOLS], F32R)
        exp_lo = sb("exp_lo", [P, SPLIT_SLOTS, ECOLS], F32R)

        with ExitStack() as early:
            qT = sb("qT", [P, HC, TOK], life=early)
            kT = sb("kT", [P, HC, TOK], life=early)
            v_s = sb("v_s", [P, STACKS, INNER], life=early)
        hid_hi = sb("hid_hi", [P, 2 * HK, SLOTS], F32R)
        hid_lo = sb("hid_lo", [P, 2 * HK, SLOTS], F32R)
        relu = sb("relu", [P, 2, TOK])
        sq = sb("sq", [P, 2, TOK])
        sb("early_rest", [P, 1000])

        wout_hi = sb("wout_hi", [P, HC, DIM], F32R)
        wout_lo = sb("wout_lo", [P, HC, DIM], F32R)
        small_s = sb("small_s", [P, SMALL])
        ones_s = sb("ones_s", [1, P])
        rows_s = sb("rows_s", [P, ROWS, DIM])
        consts_s = sb("consts_s", [P, 2 * P + SCOLS + KC * EXPERTS])
        ident_s = consts_s[:, 0:P]
        maskq_f = consts_s[:, P:2 * P]
        maskk_f = consts_s[:, 2 * P:2 * P + SCOLS]
        gate_s = consts_s[:, 2 * P + SCOLS:].rearrange("p (k e) -> p k e", k=KC)
        maskq_s = sb("maskq_s", [P, P], BF16)
        maskk_s = sb("maskk_s", [P, SCOLS], BF16)
        ang = sb("ang", [P, 6, 32])
        table = sb("table", [P, 32])
        x5 = sb("x5", [P, STACKS, DIM])
        ropa = sb("ropa", [P, STACKS, DIM])
        ropb = sb("ropb", [P, STACKS, DIM])
        h = sb("h", [P, STACKS, DIM])
        xn = sb("xn", [P, STACKS, DIM])
        power = sb("power", [P, STACKS])
        ssq = sb("ssq", [P, STACKS])
        var = sb("var", [P, 4, STACKS])
        rstd = sb("rstd", [P, 4, STACKS])
        stats = sb("stats", [P, STACKS, 6])
        mv = sb("mv", [P, 3, STACKS, 2])
        xT_hi = sb("xT_hi", [P, KC, SLOTS], F32R)
        xT_lo = sb("xT_lo", [P, KC, SLOTS], F32R)
        hb = sb("hb", [P, STACKS, DIM])
        prob = sb("prob", [P, DEPTH, Q4 * 2, 32])
        probT = sb("probT", [P, DEPTH, Q4 * 2, 32])
        smax = sb("smax", [P, DEPTH, Q4 * 2])
        ssum = sb("ssum", [P, DEPTH, Q4 * 2])
        gate_hi = sb("gate_hi", [P, KC, EXPERTS], F32R)
        gate_lo = sb("gate_lo", [P, KC, EXPERTS], F32R)
        zeros = sb("zeros", [P, BANK], BF16)
        logit = sb("logit", [P, STACKS, EXPERTS])
        gmax = sb("gmax", [P, STACKS])
        gsum = sb("gsum", [P, STACKS])
        gprob = sb("gprob", [P, STACKS, 16])
        gtop = sb("gtop", [P, STACKS, 8])
        gfind = sb("gfind", [P, STACKS, 8])
        gleft = sb("gleft", [P, STACKS, 16])
        comb = sb("comb", [P, STACKS, EXPERTS])

        ps = ctx.enter_context(nc.psum_tensor("ps", [P, 8, BANK], F32))

        ld_x = [sem(f"ld_x{c}") for c in range(C_PARTS)]
        ld_small, ld_w2, ld_w3, ld_w45 = sem("ld_small"), sem("ld_w2"), sem("ld_w3"), sem("ld_w45")
        ld_rows, ld_consts = sem("ld_rows"), sem("ld_consts")
        ld_qkv = [sem(f"ld_qkv{i}") for i in range(6)]
        ld_raw = [sem(f"ld_raw{i}") for i in range(RAW_SLOTS)]
        pad_zero, end_zero = sem("pad_zero"), sem("end_zero")
        const_ready, prob_zero = sem("const_ready"), sem("prob_zero")
        conv1_mm, conv1_act = sem("conv1_mm"), sem("conv1_act")
        conv2_mm, conv2_act = sem("conv2_mm"), sem("conv2_act")
        conv3_mm, conv3_act = sem("conv3_mm"), sem("conv3_act")
        conv4_mm, conv4_act = sem("conv4_mm"), sem("conv4_act")
        conv5_mm, conv5_act = sem("conv5_mm"), sem("conv5_act")
        angle, sines, table_ready = sem("angle"), sem("sines"), sem("table_ready")
        gate_split, zeros_ready = sem("gate_split"), sem("zeros_ready")
        rope_part, rope_y = sem("rope_part"), sem("rope_y")
        squares, rstd_var = sem("squares"), sem("rstd_var")
        root = [sem(f"root{i}") for i in range(4)]
        stat_ready = [None] + [sem(f"stat_ready{i}") for i in range(1, 4)]
        mv_ready = [None] + [sem(f"mv_ready{i}") for i in range(1, 4)]
        h_ready = sem("h_ready")
        xn_ready, xT_mm, xT_high, xT_low = sem("xn_ready"), sem("xT_mm"), sem("xT_high"), sem("xT_low")
        raw_low_pool = sem("raw_low_pool")
        qkv_high, qkv_low, qkv_low_pool = sem("qkv_high"), sem("qkv_low"), sem("qkv_low_pool")
        proj_mm, proj_out = sem("proj_mm"), sem("proj_out")
        score_mm, s_max, s_shift, s_exp = sem("score_mm"), sem("s_max"), sem("s_shift"), sem("s_exp")
        s_sum, s_inv, s_norm, s_turn = sem("s_sum"), sem("s_inv"), sem("s_norm"), sem("s_turn")
        pv_mm, att_high, att_low, att_zero = sem("pv_mm"), sem("att_high"), sem("att_low"), sem("att_zero")
        out_mm, out_read, hb_ready = sem("out_mm"), sem("out_read"), sem("hb_ready")
        raw_high, raw_low = sem("raw_high"), sem("raw_low")
        gate_mm, g_step, g_exp, comb_ready = sem("gate_mm"), sem("g_step"), sem("g_exp"), sem("comb_ready")
        up_mm, relu_done, sq_done = sem("up_mm"), sem("relu_done"), sem("sq_done")
        hid_high, hid_low = sem("hid_high"), sem("hid_low")
        down_mm, mixed = sem("down_mm"), sem("mixed")
        stored, stored_pool = sem("stored"), sem("stored_pool")

        def v(s, *halves):
            return ("project", [("v", s, half) for half in halves])

        def qk(p, first=0, end=4):
            return ("project", [(kind, hc) for hc in (2 * p, 2 * p + 1) for kind in "qk"][first:end])

        plan = [v(0, 0), ("turn 1", 1), v(0, 1), ("turn 1", 2), qk(0), qk(1, 0, 1),
                ("scores", 0), qk(1, 1, 4), qk(2, 0, 1),
                ("scores", 1), qk(2, 1, 4), qk(3, 0, 1),
                ("scores", 2), qk(3, 1, 2), ("pv", 0), qk(3, 2, 4),
                ("scores", 3), v(1, 0), ("pv", 1), v(1, 1),
                ("scores", 4), v(2, 0), ("pv", 2), v(2, 1),
                ("scores", 5), ("pv", 3),
                ("scores", 6), ("pv", 4),
                ("scores", 7), ("pv", 5),
                ("scores", 8), ("pv", 6),
                ("scores", 9), ("pv", 7),
                ("scores", 10), ("pv", 8),
                ("scores", 11), ("pv", 9), ("finish", 11), ("out", 0), ("pv", 10), ("pv", 11), ("clear", 0), ("residual", 0),
                ("normalize", 0), ("out", 1), ("turn 2", 0), ("residual", 1), ("normalize", 1), ("out", 2),
                ("turn 2", 1)]
        items = [it for what, some in plan if what == "project" for it in some]
        item_at = {it: i for i, it in enumerate(items)}

        def done_before(kind, step):
            return sum(what == kind for what, _ in plan[:plan.index(step)])

        piece_order = [4, 5, 0, 2, 1, 3]
        DVE_LOW = 4

        def piece_of(it):
            if it[0] == "v":
                return 4 + it[2]
            return (0 if it[0] == "q" else 2) + it[1] // 4

        split_after = {u: [] for u in range(UNITS)}
        for n in range(PIECES * (1 + SPLIT_SLOTS)):
            split_after[n if n < PIECES else PIECES + 1 + (n - PIECES) // 2].append(divmod(n, PIECES))

        def for_pool(j, piece):
            return 1 <= j <= SPLIT_SLOTS and piece % 2 == 1

        def low_count(j, pieces, of_pool):
            order = [divmod(n, PIECES) for n in range(PIECES * j + pieces)]
            return sum(for_pool(*it) == of_pool for it in order)

        def steps_of(u):
            at = plan.index(("scores", u))
            end = plan.index(("scores", u + 1)) if u + 1 < UNITS else len(plan)
            return plan[at + 1:end]

        def moving(x, kc, first=0, end=GROUPS):
            return x[:, kc, :].rearrange("p (g t) -> p g t", t=32)[:, first:end, 0:GT]

        def down_at(e, s):
            if e == EXPERTS - 1:
                return ps[:, (6, 7, 0)[s], 0:DIM]
            return ps[:, 4 + 2 * (e % 2) + s // 2, DIM * (s % 2):DIM * (s % 2) + DIM]

        def pads(x):
            g = x.rearrange("p n (g t) -> p n g t", t=32)
            return g[:, :, 0:GROUPS, GT:], g[:, :, GROUPS, :]

        def product(pe, dst, pairs, start=True):
            for i, ((w_hi, w_lo), (x_hi, x_lo)) in enumerate(pairs):
                pe.matmul(dst, w_hi, x_hi, start=(start and i == 0), stop=False)
                pe.matmul(dst, w_hi, x_lo, start=False, stop=False)
                last = pe.matmul(dst, w_lo, x_hi, start=False, stop=(i == len(pairs) - 1))
            return last

        def att_copy(dst, u):
            s, p, quads = unit_of(u)
            base = pv_bank(u)
            d = dst[:, 2 * p:2 * p + 2, P * s:P * (s + 1)].rearrange("p c (q i) -> p q c i", q=Q4)
            a = ps[:, base:base + Q4, 0:SCOLS].rearrange("p q (c t) -> p q c t", t=GT)
            return d[:, 0:quads, :, 0:GT], a[:, 0:quads]

        out_rows = out.rearrange("b t d -> (b t) d")
        block = ctx.enter_context(nc.Block())

        @block.sync
        def _(sp):
            for c in range(C_PARTS):
                a = slice(P + BANK * c if c else 0, P + BANK * (c + 1))
                sp.dma_start(xw_s[:, a], xw[:, a]).then_inc(ld_x[c], 16)
                if c == 0:
                    sp.dma_start(small_s[:], small).then_inc(ld_small, 16)
            sp.dma_start(w2_s[:], w2).then_inc(ld_w2, 16)
            sp.dma_start(w3_s[:], w3).then_inc(ld_w3, 16)
            qkv_v = w_qkv.rearrange("(k p) n -> p k n", p=P)

            def load_qkv(some):
                for i in some:
                    a = slice(BANK * i, BANK * (i + 1))
                    sp.dma_start(qkv_raw[:, :, a], qkv_v[:, :, a]).then_inc(ld_qkv[i], 16)

            load_qkv(piece_order[0:2])
            sp.dma_start(w45_s[:], w45).then_inc(ld_w45, 16)
            sp.dma_start(rows_s[:].rearrange("p a b -> p (a b)"), rows.broadcast_to([P, ROWS * DIM])).then_inc(ld_rows, 16)
            load_qkv(piece_order[2:6])
            sp.dma_start(consts_s[:], consts).then_inc(ld_consts, 16)
            sp.wait_ge(conv5_mm, STACKS)
            for j in range(EXPERTS + 1):
                slot = j % RAW_SLOTS
                if j >= RAW_SLOTS:
                    sp.wait_ge(raw_high, PIECES * (j - RAW_SLOTS + 1))
                    sp.wait_ge(raw_low, low_count(j - RAW_SLOTS, PIECES, False))
                    if j > RAW_SLOTS:
                        sp.wait_ge(raw_low_pool, low_count(j - RAW_SLOTS, PIECES, True))
                if j == 0:
                    sp.dma_start(raw[:, slot, :].rearrange("p (k d) -> p k d", k=HC),
                                 w_out.rearrange("(k p) d -> p k d", p=P)).then_inc(ld_raw[slot], 32)
                    continue
                e = j - 1
                sp.dma_start(raw[:, slot, 0:KC * HIDDEN].rearrange("p (k n) -> p k n", k=KC),
                             W1[e].rearrange("(k p) n -> p k n", p=P)).then_inc(ld_raw[slot], 16)
                sp.dma_start(raw[:, slot, KC * HIDDEN:].rearrange("p (k n) -> p k n", k=HK),
                             W2[e].rearrange("(k p) n -> p k n", p=P)).then_inc(ld_raw[slot], 16)
            for g in range(GROUPS):
                s, q = divmod(g, Q4)
                if g in POOL_STORES:
                    continue
                sp.wait_ge(mixed, STACKS * (EXPERTS - 1) + s + 1)
                n = min(GT, CLIPS * FRAMES - GT * g)
                sp.dma_start(out_rows[GT * g:GT * g + n, :], h[32 * q:32 * q + n, s, :]).then_inc(stored, 16)
            by_pool = len(POOL_STORES)
            sp.wait_ge(stored, 16 * (GROUPS - by_pool))
            sp.wait_ge(stored_pool, 16 * by_pool)

        @block.tensor
        def _(pe):
            def keep_warm(n, bank, columns=BANK):
                for _ in range(n):
                    pe.matmul(ps[:, bank, 0:columns], zeros[:, 0:P], zeros[:, 0:columns], start=True, stop=True)

            pe.wait_ge(zeros_ready, 1)
            keep_warm(WARM[0], 7)
            for c in range(C_PARTS):
                pe.wait_ge(ld_x[c], 16)
                pe.matmul(ps[:, c, :], xw_s[:, 0:P], xw_s[:, P + BANK * c:P + BANK * (c + 1)], start=True, stop=True)\
                  .then_inc(conv1_mm, 1)
            pe.wait_ge(ld_w2, 16)
            pe.wait_ge(pad_zero, 1)
            pe.wait_ge(end_zero, 1)
            h1_blocks = h1[:].rearrange("p (w b) -> p w b", b=CLIPS)
            for c in range(C_PARTS):
                pe.wait_ge(conv1_act, c + 1)
                for b in range(3):
                    at = C1_STEP * c + b
                    mm = pe.matmul(ps[:, 3 + c, 0:BANK // 2], w2_s[:, b, :], h1_blocks[:, at:at + C1_STEP - 1:2, :],
                                   start=(b == 0), stop=(b == 2))
                mm.then_inc(conv2_mm, 1)
            keep_warm(WARM[1], 7)
            pe.wait_ge(ld_w3, 16)
            pe.wait_ge(pad_zero, 3)
            pe.wait_ge(conv2_act, C_PARTS)
            for m in range(KC):
                dst = ps[:, 6 + m, 0:FRAMES * CLIPS].rearrange("p (t b) -> p t b", b=CLIPS)
                for odd in range(PARITIES):
                    for j in range(PAIRS):
                        rows_ = slice(0, P if odd or j < PAIRS - 1 else C2)
                        first = S3 * odd // 2 + j
                        frames = FRAMES // 2 + 1 - odd
                        mm = pe.matmul(dst[:, odd::2, :], w3_s[rows_, odd, j, P * m:P * (m + 1)],
                                       h2[rows_, first:first + S3 * (frames - 1) + 1:S3, :],
                                       start=(j == 0), stop=(j == PAIRS - 1))
                mm.then_inc(conv3_mm, 1)
            pe.wait_ge(ld_w45, 16)
            for m in range(KC):
                pe.wait_ge(conv3_act, m + 1)
                for j in range(3):
                    mm = pe.matmul(ps[:, m, 0:FRAMES * CLIPS], w4_s[:, m, j, :], h3[:, m, j:j + FRAMES, :],
                                   start=(j == 0), stop=(j == 2))
                mm.then_inc(conv4_mm, 1)
            pe.wait_ge(const_ready, 1)
            pe.wait_ge(ld_rows, 16)
            for s in range(STACKS):
                pe.matmul(ps[:, 2 + s, 0:DIM], ones_s[:], rows_s[0:1, ROW_B5, :], start=True, stop=False)
            pe.wait_ge(conv4_act, KC)
            for s in range(STACKS):
                for k in range(KC):
                    mm = pe.matmul(ps[:, 2 + s, 0:DIM], h4[:, k, P * s:P * (s + 1)], w5_s[:, k, :],
                                   start=False, stop=(k == KC - 1))
                mm.then_inc(conv5_mm, 1)

            def turn(n, s, bank):
                pe.wait_ge(xn_ready, STACKS * n + s + 1)
                for k in range(KC):
                    mm = pe.transpose(ps[:, bank, P * k:P * (k + 1)], xn[:, s, P * k:P * (k + 1)], ident_s)
                mm.then_inc(xT_mm, 1)

            def split_ready(n):
                pe.wait_ge(xT_high, n)
                pe.wait_ge(xT_low, n)

            def project(some):
                for it in some:
                    i = item_at[it]
                    piece = piece_order.index(piece_of(it)) + 1
                    pe.wait_ge(qkv_high, piece)
                    if piece <= DVE_LOW:
                        pe.wait_ge(qkv_low, piece)
                    else:
                        pe.wait_ge(qkv_low_pool, piece - DVE_LOW)
                    if i >= 4:
                        pe.wait_ge(proj_out, i - 3)
                    bank = PROJ_BANK + i % 4
                    if it[0] == "v":
                        _, s, half = it
                        at = 2 * INNER + half * BANK
                        mm = product(pe, ps[:, bank, :],
                                     [((xT_hi[:, k, P * s:P * (s + 1)], xT_lo[:, k, P * s:P * (s + 1)]),
                                       (qkv_hi[:, k, at:at + BANK], qkv_lo[:, k, at:at + BANK])) for k in range(KC)])
                    else:
                        at = (0 if it[0] == "q" else INNER) + it[1] * P
                        mm = product(pe, ps[:, bank, 0:TOK],
                                     [((qkv_hi[:, k, at:at + P], qkv_lo[:, k, at:at + P]),
                                       (moving(xT_hi, k), moving(xT_lo, k))) for k in range(KC)])
                    mm.then_inc(proj_mm, 1)

            def scores(u):
                s, p, quads = unit_of(u)
                if s == 0:
                    pe.wait_ge(proj_out, item_at[("k", 2 * p + 1)] + 1)
                if u >= 1:
                    pe.wait_ge(s_shift, u)
                shared = min(SHARED_PV, done_before("pv", ("scores", u)))
                if shared and u <= SHARED_PV + 2:
                    pe.wait_ge(att_high, shared)
                    pe.wait_ge(att_low, shared)
                for b in range(Q4):
                    pe.matmul(ps[:, b, 0:SCOLS], maskq_s[32 * b:32 * b + GROUP_CLIPS, :],
                              maskk_s[32 * b:32 * b + GROUP_CLIPS, :], start=True, stop=True)
                for hcl in range(2):
                    for q in range(quads):
                        g = Q4 * s + q
                        for b in range(Q4):
                            rows_ = slice(32 * b, 32 * b + 32)
                            mm = pe.matmul(ps[32 * q:32 * q + GT, b, GT * hcl:GT * (hcl + 1)],
                                           qT[rows_, 2 * p + hcl, GT * g:GT * (g + 1)],
                                           kT[rows_, 2 * p + hcl, GT * g:GT * (g + 1)],
                                           start=False, stop=True, skip_group_check=True)
                mm.then_inc(score_mm, 1)

            def pv(u):
                s, p, quads = unit_of(u)
                pe.wait_ge(s_turn, u + 1)
                if p == 0:
                    pe.wait_ge(proj_out, item_at[("v", s, 1)] + 1)
                if quads == Q4 and done_before("out", ("pv", u)):
                    pe.wait_ge(out_read, done_before("out", ("pv", u)))
                if u < SHARED_PV:
                    pe.wait_ge(s_shift, done_before("scores", ("pv", u)))
                elif u == SHARED_PV:
                    pe.wait_ge(proj_out, len(items))
                elif u == UNITS - 2:
                    pe.wait_ge(s_shift, UNITS)
                else:
                    pe.wait_ge(att_high, u if u < UNITS - 2 else u - 1)
                    pe.wait_ge(att_low, u if u < UNITS - 2 else u - 1)
                base = pv_bank(u)
                for hcl in range(2):
                    for b in range(Q4):
                        head = 4 * (2 * p + hcl) + b
                        for q in range(quads):
                            mm = pe.matmul(ps[32 * b:32 * b + 32, base + q, GT * hcl:GT * (hcl + 1)],
                                           v_s[32 * q:32 * q + GT, s, 32 * head:32 * head + 32],
                                           probT[32 * q:32 * q + GT, u % DEPTH, 2 * b + hcl, 0:GT],
                                           start=True, stop=True)
                mm.then_inc(pv_mm, 1)

            def out_project(s):
                pe.wait_ge(att_high, PAIR_COUNT * (s + 1))
                pe.wait_ge(att_low, PAIR_COUNT * (s + 1))
                if s == 0:
                    pe.wait_ge(raw_high, PIECES)
                    pe.wait_ge(raw_low, PIECES)
                if OUT_BANK[s] == 7:
                    with_quad_3 = min(done_before("pv", ("out", s)), (GROUPS // Q4) * PAIR_COUNT)
                    pe.wait_ge(att_high, with_quad_3)
                    pe.wait_ge(att_low, with_quad_3)
                else:
                    pe.wait_ge(s_shift, UNITS)
                a = slice(P * s, P * (s + 1))
                dst = ps[:, OUT_BANK[s], 0:DIM]
                pe.matmul(dst, ones_s[:], rows_s[0:1, ROW_BOUT, :], start=True, stop=False)
                product(pe, dst, [((att_hi[:, hc, a], att_lo[:, hc, a]), (wout_hi[:, hc, :], wout_lo[:, hc, :]))
                                  for hc in range(HC)], start=False).then_inc(out_mm, 1)

            pe.wait_ge(ld_consts, 16)
            keep_warm(WARM[2], 7)
            turn(0, 0, 0)
            keep_warm(WARM[3], 7)
            split_ready(1)
            for what, arg in plan:
                if what == "turn 1":
                    turn(0, arg, arg)
                elif what == "project":
                    if arg[0] == ("q", 0):
                        split_ready(STACKS)
                    if arg[0][0] == "v":
                        split_ready(arg[0][1] + 1)
                    project(arg)
                elif what == "scores":
                    if arg == 0:
                        pe.wait_ge(const_ready, 2)
                    scores(arg)
                elif what == "pv":
                    pv(arg)
                elif what == "turn 2":
                    pe.wait_ge(out_read, 1)
                    if arg:
                        split_ready(STACKS + arg)
                        keep_warm(WARM[4], 5)
                    turn(1, arg, TURN_BANK[arg])
                elif what == "out":
                    out_project(arg)

            def up(e, first=0, end=GROUPS):
                pe.wait_ge(raw_high, PIECES * (e + 1) + PIECES // 2)
                pe.wait_ge(raw_low, low_count(e + 1, PIECES // 2, False))
                pe.wait_ge(raw_low_pool, low_count(e + 1, PIECES // 2, True))
                slot = e % SPLIT_SLOTS
                last = first > 0
                for m in range(HK):
                    n = HK * e + m
                    if n >= 4 and first == 0:
                        pe.wait_ge(relu_done, n - 3)
                    if n == 3:
                        pe.wait_ge(out_read, STACKS)
                    pairs = []
                    for k in range(KC):
                        at = k * HIDDEN + P * m
                        x = [t[:, k, 32 * first:] if last else moving(t, k, first, end) for t in (xT_hi, xT_lo)]
                        pairs.append(((exp_hi[:, slot, at:at + P], exp_lo[:, slot, at:at + P]), x))
                    mm = product(pe, ps[:, UP_BANK[n % 4], GT * first:GT * first + P if last else GT * end], pairs)
                    if end == GROUPS:
                        mm.then_inc(up_mm, 1)

            def gate(s):
                a = slice(P * s, P * (s + 1))
                product(pe, ps[:, 6, EXPERTS * s:EXPERTS * (s + 1)],
                        [((xT_hi[:, k, a], xT_lo[:, k, a]), (gate_hi[:, k, :], gate_lo[:, k, :]))
                         for k in range(KC)]).then_inc(gate_mm, 1)

            def down(e):
                pe.wait_ge(hid_high, HK * (e + 1))
                pe.wait_ge(hid_low, HK * (e + 1))
                if e >= 2:
                    pe.wait_ge(mixed, STACKS * (e - 1))
                pe.wait_ge(raw_high, PIECES * (e + 2))
                pe.wait_ge(raw_low, low_count(e + 1, PIECES, False))
                pe.wait_ge(raw_low_pool, low_count(e + 1, PIECES, True))
                slot = e % SPLIT_SLOTS
                for s in range(STACKS):
                    pairs = []
                    for k in range(HK):
                        at = KC * HIDDEN + k * DIM
                        n = HK * (e % 2) + k
                        pairs.append(((hid_hi[:, n, P * s:P * (s + 1)], hid_lo[:, n, P * s:P * (s + 1)]),
                                      (exp_hi[:, slot, at:at + DIM], exp_lo[:, slot, at:at + DIM])))
                    product(pe, down_at(e, s), pairs).then_inc(down_mm, 1)

            keep_warm(WARM[5], 5)
            split_ready(STACKS + 2)
            up(0, 0, 2 * Q4)
            turn(1, 2, TURN_BANK[2])
            pe.wait_ge(gate_split, 2)
            gate(0)
            gate(1)
            split_ready(STACKS + 3)
            up(0, 2 * Q4, GROUPS)
            gate(2)
            for e in range(EXPERTS):
                if e + 1 < EXPERTS:
                    up(e + 1)
                if e == 1:
                    pe.wait_ge(g_step, 1)
                down(e)

        @block.scalar
        def _(act):
            b1 = small_s[:, COL_B1:COL_B1 + 1]
            act.wait_ge(ld_small, 16)
            for c in range(C_PARTS):
                act.wait_ge(conv1_mm, c + 1)
                at, n = (C1_STEP * c + 1) * CLIPS, BANK
                if c == C_PARTS - 1:
                    n = BANK - CLIPS
                    act.activation(h1[0:64, at + n:at + BANK], ps[0:64, c, n:BANK], ACT.Gelu, bias=b1[0:64, :])
                act.activation(h1[:, at:at + n], ps[:, c, 0:n], ACT.Gelu, bias=b1).then_inc(conv1_act, 1)
            act.wait_ge(pad_zero, 2)
            for c in range(C_PARTS):
                act.wait_ge(conv2_mm, c + 1)
                at = (PAD3 + C1_STEP * c) // 2
                act.activation(h2[:, at:at + C1_STEP // 2, :].rearrange("p a b -> p (a b)"), ps[:, 3 + c, 0:BANK // 2],
                               ACT.Gelu, bias=small_s[:, COL_B2:COL_B2 + 1]).then_inc(conv2_act, 1)
            act.wait_ge(angle, 8)
            act.activation(table[:], ang[:, 5, :], ACT.Sin).then_inc(sines, 1)
            for m in range(KC):
                act.wait_ge(conv3_mm, m + 1)
                act.activation(h3[:, m, 1:1 + FRAMES, :].rearrange("p a b -> p (a b)"), ps[:, 6 + m, 0:FRAMES * CLIPS],
                               ACT.Gelu, bias=small_s[:, COL_B3 + m:COL_B3 + m + 1]).then_inc(conv3_act, 1)
            act.wait_ge(pad_zero, 4)
            for m in range(KC):
                act.wait_ge(conv4_mm, m + 1)
                bias = small_s[:, COL_B4 + m:COL_B4 + m + 1]
                src = ps[:, m, 0:FRAMES * CLIPS].rearrange("p (t b) -> p b t", t=FRAMES)
                dst = h4[:, m, :].rearrange("p (g i) -> p g i", i=32)
                full = FULL_GROUPS * GROUP_CLIPS
                act.activation(dst[:, 0:FULL_GROUPS, 0:GT].rearrange("p g (b t) -> p g b t", t=FRAMES),
                               src[:, 0:full, :].rearrange("p (g b) t -> p g b t", b=GROUP_CLIPS), ACT.Gelu, bias=bias)
                act.activation(dst[:, FULL_GROUPS, 0:REST_CLIPS * FRAMES].rearrange("p (b t) -> p b t", t=FRAMES),
                               src[:, full:CLIPS, :], ACT.Gelu, bias=bias).then_inc(conv4_act, 1)
            for s in range(STACKS):
                act.wait_ge(conv5_mm, s + 1)
                act.activation(x5[:, s, :], ps[:, 2 + s, 0:DIM], ACT.Gelu).then_inc(conv5_act, 1)
            for s in range(STACKS):
                act.wait_ge(rope_y, s + 1)
                act.activation(xn[:, s, :], ropa[:, s, :], ACT.Square, accum_out=ssq[:, s:s + 1]).then_inc(squares, 1)

            def turned(n, s, bank):
                act.wait_ge(xT_mm, STACKS * n + s + 1)
                src = ps[:, bank, 0:KC * P].rearrange("p (k i) -> p k i", k=KC)
                act.activation(xT_hi[:, :, P * s:P * (s + 1)], src, ACT.Copy).then_inc(xT_high, 1)

            def copy_out(some):
                for it in some:
                    i = item_at[it]
                    act.wait_ge(proj_mm, i + 1)
                    bank = PROJ_BANK + i % 4
                    if it[0] == "v":
                        dst, src = v_s[:, it[1], BANK * it[2]:BANK * (it[2] + 1)], ps[:, bank, :]
                    else:
                        dst, src = (qT if it[0] == "q" else kT)[:, it[1], :], ps[:, bank, 0:TOK]
                    act.activation(dst, src, ACT.Copy).then_inc(proj_out, 1)

            def exponentials(u):
                act.wait_ge(s_shift, u + 1)
                e = prob[:, u % DEPTH, :, 0:GT]
                act.activation(e, e, ACT.Exp, scale=SCALE).then_inc(s_exp, 1)

            def attended(u):
                act.wait_ge(pv_mm, u + 1)
                if u == 0:
                    act.wait_ge(att_zero, 1)
                dst, src = att_copy(att_hi, u)
                act.activation(dst, src, ACT.Copy).then_inc(att_high, 1)

            def split(j, piece):
                act.wait_ge(ld_raw[j % RAW_SLOTS], 32 * (j // RAW_SLOTS + 1))
                if j >= 1:
                    if j <= SPLIT_SLOTS:
                        act.wait_ge(proj_mm, len(items))
                    else:
                        act.wait_ge(down_mm, STACKS * (j - SPLIT_SLOTS))
                a = slice(PIECE * piece, PIECE * (piece + 1))
                dst = wout_hi[:].rearrange("p k d -> p (k d)") if j == 0 else exp_hi[:, (j - 1) % SPLIT_SLOTS, :]
                act.activation(dst[:, a], raw[:, j % RAW_SLOTS, a], ACT.Copy).then_inc(raw_high, 1)

            def follow(steps):
                for what, arg in steps:
                    if what == "project":
                        copy_out(arg)
                    elif what == "turn 1":
                        turned(0, arg, arg)
                    elif what == "pv":
                        attended(arg)
                    elif what == "turn 2":
                        turned(1, arg, TURN_BANK[arg])

            turned(0, 0, 0)
            follow(plan[:plan.index(("scores", 0))])
            for u in range(UNITS):
                exponentials(u)
                follow(steps_of(u))
                for j, piece in split_after[u]:
                    split(j, piece)
            turned(1, 2, TURN_BANK[2])

            for e in range(EXPERTS):
                for m in range(HK):
                    n = HK * e + m
                    act.wait_ge(up_mm, n + 1)
                    if n >= 2:
                        act.wait_ge(sq_done, n - 1)
                        act.wait_ge(hid_high, n - 1)
                    ahead = TOK if e else 2 * Q4 * GT
                    if e == 0:
                        act.activation(relu[:, n % 2, ahead:].rearrange("p (g t) -> p g t", t=GT),
                                       ps[:, UP_BANK[n % 4], ahead:ahead + P].rearrange("p (g t) -> p g t", t=32)
                                       [:, 0:GROUPS - 2 * Q4, 0:GT], ACT.Relu)
                    act.activation(relu[:, n % 2, 0:ahead], ps[:, UP_BANK[n % 4], 0:ahead], ACT.Relu).then_inc(relu_done, 1)
                    act.wait_ge(relu_done, n + 1)
                    if e >= 2:
                        act.wait_ge(down_mm, STACKS * (e - 1))
                    if n == 0:
                        act.wait_ge(pad_zero, 5)
                    dst = hid_hi[:, n % (2 * HK), :].rearrange("p (g t) -> p g t", t=32)[:, 0:GROUPS, 0:GT]
                    act.activation(dst, relu[:, n % 2, :].rearrange("p (g t) -> p g t", t=GT), ACT.Square)\
                       .then_inc(hid_high, 1)
                if e == 0:
                    act.wait_ge(g_step, 3)
                    act.activation(logit[:], logit[:], ACT.Exp).then_inc(g_exp, 1)
                if e >= 1 and e + 3 <= EXPERTS:
                    for piece in range(PIECES):
                        split(e + 3, piece)

        @block.gpsimd
        def _(pool):
            pool.memset(h1[:, 0:CLIPS], 0.0).then_inc(pad_zero, 1)
            pool.memset(h2[:, 0:PAD3 // 2, :], 0.0)
            pool.memset(h2[:, H2_COLS - 1:, :], 0.0).then_inc(pad_zero, 1)
            pool.memset(h3[:, :, 0:FRAMES + 2:FRAMES + 1, :], 0.0).then_inc(pad_zero, 1)
            pool.memset(h4[:], 0.0).then_inc(pad_zero, 1)
            pool.memset(ones_s[:], 1.0).then_inc(const_ready, 1)
            pool.memset(power[:], -0.5)
            pool.memset(gprob[:], -1.0)
            pool.memset(gfind[:], -1.0)
            pool.memset(prob[:], 0.0).then_inc(prob_zero, 1)
            for n, i in list(enumerate(piece_order))[DVE_LOW:]:
                a = slice(BANK * i, BANK * (i + 1))
                pool.wait_ge(qkv_high, n + 1)
                pool.tensor_tensor(qkv_lo[:, :, a], qkv_raw[:, :, a], qkv_hi[:, :, a].bitcast(F32), ALU.subtract)\
                    .then_inc(qkv_low_pool, 1)

            n_root = [0]

            def inverse_root(kind, s, src, scale, eps):
                pool.tensor_scalar(var[:, kind, s:s + 1], src, scale, eps, ALU.mult, ALU.add).then_inc(rstd_var, 1)
                n_root[0] += 1
                pool.wait_ge(rstd_var, n_root[0])
                pool.tensor_tensor(rstd[:, kind, s:s + 1], var[:, kind, s:s + 1], power[:, 0:1], ALU.pow)\
                    .then_inc(root[kind], 1)

            def rms_root(s):
                pool.wait_ge(squares, s + 1)
                inverse_root(0, s, ssq[:, s:s + 1], 1.0 / DIM, RMS_EPS)

            def ln_root(kind, s):
                pool.wait_ge(mv_ready[kind], s + 1)
                inverse_root(kind, s, mv[:, kind - 1, s, 1:2], 1.0, ATT_EPS if kind == 2 else LN_EPS)

            rms_root(0)
            rms_root(1)
            ln_root(1, 0)
            rms_root(2)
            ln_root(1, 1)
            ln_root(1, 2)
            pool.wait_ge(ld_consts, 16)
            pool.tensor_copy(maskq_s[:], maskq_f)
            pool.tensor_copy(maskk_s[:], maskk_f).then_inc(const_ready, 1)
            pool.wait_ge(qkv_low, DVE_LOW)
            pool.wait_ge(qkv_low_pool, len(piece_order) - DVE_LOW)
            for x in (att_hi, att_lo):
                for pad in pads(x[:].bitcast(F32)):
                    ms = pool.memset(pad, 0.0)
            ms.then_inc(att_zero, 1)
            for s in range(STACKS):
                pool.tensor_tensor(hb[:, s, :], h[:, s, :], rows_s[:, ROW_BETA, :], ALU.add).then_inc(hb_ready, 1)

            def normed(u):
                pool.wait_ge(s_inv, u + 1)
                e = prob[:, u % DEPTH, :, 0:GT]
                pool.tensor_tensor(e, e, ssum[:, u % DEPTH, :, None].broadcast_to([P, Q4 * 2, GT]), ALU.mult)\
                    .then_inc(s_norm, 1)

            def split(j, piece):
                a = slice(PIECE * piece, PIECE * (piece + 1))
                slot = (j - 1) % SPLIT_SLOTS
                pool.wait_ge(raw_high, PIECES * j + piece + 1)
                pool.tensor_tensor(exp_lo[:, slot, a], raw[:, j % RAW_SLOTS, a], exp_hi[:, slot, a].bitcast(F32),
                                   ALU.subtract).then_inc(raw_low_pool, 1)

            for u in range(UNITS):
                if u:
                    normed(u - 1)
                    for j, piece in split_after[u - 1]:
                        if for_pool(j, piece):
                            split(j, piece)
                for what, arg in steps_of(u):
                    if what == "out" and arg < STACKS - 1:
                        ln_root(2, arg)
                    elif what == "residual":
                        ln_root(3, arg)
                    elif what == "finish":
                        normed(arg)
                    elif what == "clear":
                        pool.wait_ge(pv_mm, UNITS)
                        for x in (hid_hi, hid_lo):
                            for pad in pads(x[:].bitcast(F32)):
                                ms = pool.memset(pad, 0.0)
                        ms.then_inc(pad_zero, 1)
            ln_root(2, 2)
            ln_root(3, 2)
            for n in range(HK * EXPERTS):
                pool.wait_ge(relu_done, n + 1)
                if n >= 2:
                    pool.wait_ge(hid_low, n - 1)
                pool.tensor_tensor(sq[:, n % 2, :], relu[:, n % 2, :], relu[:, n % 2, :], ALU.mult).then_inc(sq_done, 1)
            for g in range(GROUPS):
                s, q = divmod(g, Q4)
                if g in POOL_STORES:
                    pool.wait_ge(mixed, STACKS * (EXPERTS - 1) + s + 1)
                    n = min(GT, CLIPS * FRAMES - GT * g)
                    pool.dma_start(out_rows[GT * g:GT * g + n, :], h[32 * q:32 * q + n, s, :]).then_inc(stored_pool, 16)

        @block.vector
        def _(dve):
            dve.memset(zeros[:], 0.0).then_inc(zeros_ready, 1)
            dve.memset(h1[64:P, BLOCKS * CLIPS:], 0.0).then_inc(end_zero, 1)
            dve.wait_ge(ld_small, 16)
            phase = small_s[:, COL_PHASE:COL_PHASE + 32]
            n_angle = [0]

            def angle_step(ins):
                n_angle[0] += 1
                ins.then_inc(angle, 1)
                dve.wait_ge(angle, n_angle[0])

            angle_step(dve.tensor_scalar(ang[:, 0, :], small_s[:, COL_FREQ:COL_FREQ + 32],
                                         small_s[:, COL_FRAME:COL_FRAME + 1], None, ALU.mult))
            angle_step(dve.tensor_tensor(ang[:, 1, :], ang[:, 0, :], phase, ALU.add))
            angle_step(dve.tensor_scalar(ang[:, 2, :], ang[:, 1, :], 1.0 / (2 * PI), ROUNDER, ALU.mult, ALU.add))
            angle_step(dve.tensor_scalar(ang[:, 2, :], ang[:, 2, :], ROUNDER, None, ALU.subtract))
            angle_step(dve.scalar_tensor_tensor(out=ang[:, 3, :], in0=ang[:, 2, :], scalar=-TWO_PI_HI, in1=ang[:, 0, :],
                                                op0=ALU.mult, op1=ALU.add))
            angle_step(dve.scalar_tensor_tensor(out=ang[:, 4, :], in0=ang[:, 2, :], scalar=-TWO_PI_MID, in1=ang[:, 3, :],
                                                op0=ALU.mult, op1=ALU.add))
            angle_step(dve.tensor_tensor(ang[:, 3, :], ang[:, 4, :], phase, ALU.add))
            angle_step(dve.tensor_scalar(ang[:, 5, :], ang[:, 3, :], 3.1415925, -3.1415925, ALU.min, ALU.max))

            def round_qkv(n):
                a = slice(BANK * piece_order[n], BANK * (piece_order[n] + 1))
                dve.wait_ge(ld_qkv[piece_order[n]], 16)
                dve.tensor_copy(qkv_hi[:, :, a], qkv_raw[:, :, a]).then_inc(qkv_high, 1)

            def rest_qkv(n):
                a = slice(BANK * piece_order[n], BANK * (piece_order[n] + 1))
                dve.wait_ge(qkv_high, n + 1)
                dve.tensor_tensor(qkv_lo[:, :, a], qkv_raw[:, :, a], qkv_hi[:, :, a].bitcast(F32), ALU.subtract)\
                   .then_inc(qkv_low, 1)

            for n in range(DVE_LOW):
                round_qkv(n)
                rest_qkv(n)
            dve.wait_ge(sines, 1)
            dve.tensor_tensor(table[:], table[:], small_s[:, COL_SIGN:COL_SIGN + 32], ALU.mult).then_inc(table_ready, 1)
            for n in (4, 5):
                round_qkv(n)

            cos_b, sin_b = (table[:, None, i:i + 16].broadcast_to([P, 16, 16]) for i in (0, 16))
            dve.wait_ge(table_ready, 1)

            def rope_products(s):
                dve.wait_ge(conv5_act, s + 1)
                x, a, b = (t[:, s, :].rearrange("p (h d) -> p h d", d=16) for t in (x5, ropa, ropb))
                dve.tensor_tensor(a, x, cos_b, ALU.mult).then_inc(rope_part, 1)
                for i in range(2):
                    dve.tensor_tensor(b[:, :, i::2], x[:, :, 1 - i::2], sin_b[:, :, i::2], ALU.mult).then_inc(rope_part, 1)

            def rope_sum(s):
                dve.wait_ge(rope_part, 3 * (s + 1))
                dve.tensor_tensor(ropa[:, s, :], ropa[:, s, :], ropb[:, s, :], ALU.add).then_inc(rope_y, 1)

            def rms(s):
                dve.wait_ge(rope_y, s + 1)
                dve.wait_ge(root[0], s + 1)
                dve.scalar_tensor_tensor(out=h[:, s, :], in0=ropa[:, s, :], scalar=rstd[:, 0, s:s + 1],
                                         in1=rows_s[:, ROW_NORM, :], op0=ALU.mult, op1=ALU.mult).then_inc(h_ready, 1)

            def moments(kind, s, src, ready, count):
                dve.wait_ge(ready, count)
                dve.bn_stats(stats[:, s, :], src[:, s, :]).then_inc(stat_ready[kind], 1)
                dve.wait_ge(stat_ready[kind], s + 1)
                dve.bn_aggr(mv[:, kind - 1, s, :], stats[:, s, :]).then_inc(mv_ready[kind], 1)

            def normalize(kind, s):
                dve.wait_ge(root[kind], s + 1)
                dve.wait_ge(mv_ready[kind], s + 1)
                dve.tensor_scalar(xn[:, s, :], h[:, s, :], mv[:, kind - 1, s, 0:1], rstd[:, kind, s:s + 1],
                                  ALU.subtract, ALU.mult).then_inc(xn_ready, 1)

            def turned(n, s, bank):
                dve.wait_ge(xT_high, STACKS * n + s + 1)
                a = slice(P * s, P * (s + 1))
                src = ps[:, bank, 0:KC * P].rearrange("p (k i) -> p k i", k=KC)
                dve.tensor_tensor(xT_lo[:, :, a], src, xT_hi[:, :, a].bitcast(F32), ALU.subtract).then_inc(xT_low, 1)

            dve.wait_ge(ld_rows, 16)
            for s in (0, 1):
                rope_products(s)
                rope_sum(s)
            rms(0)
            moments(1, 0, h, h_ready, 1)
            rms(1)
            rope_products(2)
            normalize(1, 0)
            rope_sum(2)
            moments(1, 1, h, h_ready, 2)
            turned(0, 0, 0)
            normalize(1, 1)
            rms(2)
            moments(1, 2, h, h_ready, 3)
            normalize(1, 2)
            turned(0, 1, 1)
            turned(0, 2, 2)
            dve.tensor_copy(gate_hi[:], gate_s).then_inc(gate_split, 1)
            dve.wait_ge(gate_split, 1)
            dve.tensor_tensor(gate_lo[:], gate_s, gate_hi[:].bitcast(F32), ALU.subtract).then_inc(gate_split, 1)

            def top(u):
                dve.wait_ge(score_mm, u + 1)
                src = ps[:, 0:Q4, 0:SCOLS].rearrange("p b (c t) -> p b c t", t=GT)
                dve.tensor_reduce(smax[:, u % DEPTH].rearrange("p (b c) -> p b c", b=Q4), src, AX.X, ALU.max).then_inc(s_max, 1)

            def shift(u):
                dve.wait_ge(s_max, u + 1)
                if u == 0:
                    dve.wait_ge(prob_zero, 1)
                if u >= DEPTH:
                    dve.wait_ge(s_turn, u - DEPTH + 1)
                src = ps[:, 0:Q4, 0:SCOLS].rearrange("p b (c t) -> p b c t", t=GT)
                m = smax[:, u % DEPTH].rearrange("p (b c) -> p b c", b=Q4)
                dst = prob[:, u % DEPTH].rearrange("p (b c) t -> p b c t", b=Q4)[:, :, :, 0:GT]
                dve.tensor_tensor(dst, src, m[:, :, :, None].broadcast_to([P, Q4, 2, GT]), ALU.subtract).then_inc(s_shift, 1)

            def sums(u):
                dve.wait_ge(s_exp, u + 1)
                dve.tensor_reduce(ssum[:, u % DEPTH], prob[:, u % DEPTH, :, 0:GT], AX.X, ALU.add).then_inc(s_sum, 1)

            def inverse(u):
                dve.wait_ge(s_sum, u + 1)
                dve.reciprocal(ssum[:, u % DEPTH], ssum[:, u % DEPTH]).then_inc(s_inv, 1)

            def turn_probs(u):
                dve.wait_ge(s_norm, u + 1)
                if u >= DEPTH:
                    dve.wait_ge(pv_mm, u - DEPTH + 1)
                dve.transpose(probT[:, u % DEPTH].rearrange("p c t -> p (c t)"),
                              prob[:, u % DEPTH].rearrange("p c t -> p (c t)")).then_inc(s_turn, 1)

            def attended(u):
                dve.wait_ge(att_high, u + 1)
                (dst, src), (hi, _) = att_copy(att_lo, u), att_copy(att_hi, u)
                dve.tensor_tensor(dst, src, hi.bitcast(F32), ALU.subtract).then_inc(att_low, 1)

            def split(j, piece):
                dve.wait_ge(raw_high, PIECES * j + piece + 1)
                a = slice(PIECE * piece, PIECE * (piece + 1))
                if j == 0:
                    dst, hi = wout_lo[:].rearrange("p k d -> p (k d)"), wout_hi[:].rearrange("p k d -> p (k d)")
                else:
                    dst, hi = exp_lo[:, (j - 1) % SPLIT_SLOTS, :], exp_hi[:, (j - 1) % SPLIT_SLOTS, :]
                dve.tensor_tensor(dst[:, a], raw[:, j % RAW_SLOTS, a], hi[:, a].bitcast(F32), ALU.subtract)\
                   .then_inc(raw_low, 1)

            def centred(s):
                out_s = ps[:, OUT_BANK[s], 0:DIM]
                dve.wait_ge(out_mm, s + 1)
                dve.bn_stats(stats[:, s, :], out_s).then_inc(stat_ready[2], 1)
                dve.wait_ge(stat_ready[2], s + 1)
                dve.bn_aggr(mv[:, 1, s, :], stats[:, s, :]).then_inc(mv_ready[2], 1)
                dve.wait_ge(mv_ready[2], s + 1)
                dve.scalar_tensor_tensor(out=ropa[:, s, :], in0=out_s, scalar=mv[:, 1, s, 0:1],
                                         in1=rows_s[:, ROW_GAMMA, :], op0=ALU.subtract, op1=ALU.mult).then_inc(out_read, 1)

            def residual(s):
                dve.wait_ge(out_read, s + 1)
                dve.wait_ge(root[2], s + 1)
                dve.wait_ge(hb_ready, s + 1)
                dve.scalar_tensor_tensor(out=h[:, s, :], in0=ropa[:, s, :], scalar=rstd[:, 2, s:s + 1],
                                         in1=hb[:, s, :], op0=ALU.mult, op1=ALU.add).then_inc(h_ready, 1)
                moments(3, s, h, h_ready, STACKS + s + 1)

            for u in range(UNITS):
                top(u)
                if u >= 1:
                    sums(u - 1)
                shift(u)
                if u >= 1:
                    inverse(u - 1)
                    for j, piece in split_after[u - 1]:
                        if not for_pool(j, piece):
                            split(j, piece)
                    turn_probs(u - 1)
                for what, arg in steps_of(u):
                    if what == "pv":
                        attended(arg)
                    elif what == "out":
                        centred(arg)
                    elif what == "residual":
                        residual(arg)
                    elif what == "normalize":
                        normalize(3, arg)
                    elif what == "turn 2":
                        turned(1, arg, TURN_BANK[arg])
                    elif what == "finish":
                        sums(arg)
                        inverse(arg)
                        turn_probs(arg)
            residual(2)
            normalize(3, 2)
            turned(1, 2, TURN_BANK[2])

            def gate():
                n_gate = [0]

                def step(ins):
                    n_gate[0] += 1
                    ins.then_inc(g_step, 1)
                    dve.wait_ge(g_step, n_gate[0])

                def wide(x):
                    return x[:, :, None].broadcast_to([P, STACKS, EXPERTS])

                dve.wait_ge(gate_mm, STACKS)
                step(dve.tensor_copy(logit[:].rearrange("p s e -> p (s e)"), ps[:, 6, 0:STACKS * EXPERTS]))
                step(dve.tensor_reduce(gmax[:], logit[:], AX.X, ALU.max))
                step(dve.tensor_tensor(logit[:], logit[:], wide(gmax), ALU.subtract))
                dve.wait_ge(g_exp, 1)
                step(dve.tensor_reduce(gsum[:], logit[:], AX.X, ALU.add))
                step(dve.reciprocal(gsum[:], gsum[:]))
                probs = gprob[:, :, 0:EXPERTS]
                step(dve.tensor_tensor(probs, logit[:], wide(gsum), ALU.mult))
                for s in range(STACKS):
                    step(dve.max(gtop[:, s, :], gprob[:, s, 0:EXPERTS]))
                step(dve.tensor_copy(gfind[:, :, 0:2], gtop[:, :, 0:2]))
                for s in range(STACKS):
                    step(dve.match_replace(gleft[:, s, :], gfind[:, s, :], gprob[:, s, :], -2.0))
                step(dve.tensor_tensor(comb[:], gleft[:, :, 0:EXPERTS], probs, ALU.not_equal))
                step(dve.tensor_tensor(comb[:], comb[:], probs, ALU.mult))
                step(dve.tensor_tensor(gsum[:], gtop[:, :, 0], gtop[:, :, 1], ALU.add))
                step(dve.tensor_scalar(gsum[:], gsum[:], TOP_EPS, None, ALU.add))
                step(dve.reciprocal(gsum[:], gsum[:]))
                dve.tensor_tensor(comb[:], comb[:], wide(gsum), ALU.mult).then_inc(comb_ready, 1)

            def low_parts(e):
                for m in range(HK):
                    n = HK * e + m
                    dve.wait_ge(sq_done, n + 1)
                    dve.wait_ge(hid_high, n + 1)
                    if n == 0:
                        dve.wait_ge(pad_zero, 5)
                    hi, lo = (x[:, n % (2 * HK), :].rearrange("p (g t) -> p g t", t=32)[:, 0:GROUPS, 0:GT]
                              for x in (hid_hi, hid_lo))
                    dve.tensor_tensor(lo, sq[:, n % 2, :].rearrange("p (g t) -> p g t", t=GT), hi.bitcast(F32),
                                      ALU.subtract).then_inc(hid_low, 1)

            def mix(e):
                for s in range(STACKS):
                    dve.wait_ge(down_mm, STACKS * e + (s if e == EXPERTS - 1 else max(s, 1)) + 1)
                    if e:
                        dve.wait_ge(mixed, STACKS * (e - 1) + s + 1)
                    dve.scalar_tensor_tensor(out=h[:, s, :], in0=down_at(e, s), scalar=comb[:, s, e:e + 1], in1=h[:, s, :],
                                             op0=ALU.mult, op1=ALU.add).then_inc(mixed, 1)

            low_parts(0)
            gate()
            dve.wait_ge(comb_ready, 1)
            for e in range(EXPERTS):
                if e + 1 < EXPERTS:
                    low_parts(e + 1)
                mix(e)
                if e + 4 <= EXPERTS:
                    for piece in range(PIECES):
                        split(e + 4, piece)


_OUT = ((CLIPS, FRAMES, DIM), "float32")


def kernel(**inputs):
    import numpy as np
    import concourse.bacc as bacc
    from concourse.bass_utils import run_bass_kernel_spmd

    a = {k: np.ascontiguousarray(v) for k, v in inputs.items()}
    f = np.float32
    arrays = {}
    x = a["x"][:, 0, :]
    padded = np.zeros((CLIPS, PER * S1 * (BLOCKS - 1) + WINDOW + PAD1), f)
    padded[:, PAD1:PAD1 + x.shape[1]] = x
    windows = np.stack([padded[:, PER * S1 * w:PER * S1 * w + WINDOW].T for w in range(BLOCKS)], 1)
    w = np.zeros((WINDOW, PER, C1), f)
    for i in range(PER):
        w[S1 * i:S1 * i + K1, i, :] = a["L0_tok_w1"][:, 0, :].T
    arrays["xw"] = np.concatenate([w.reshape(WINDOW, P), windows.reshape(WINDOW, BLOCKS * CLIPS)], 1)
    slot = np.arange(P)
    small = np.zeros((P, SMALL), f)
    small[:, COL_FRAME] = slot % 32 % FRAMES
    small[:, COL_PHASE:COL_PHASE + 16] = PI / 2
    small[:, COL_SIGN:COL_SIGN + 32] = np.concatenate([np.ones(16, f), np.tile(np.array([-1.0, 1.0], f), 8)])
    mask_q, mask_k = np.zeros((P, P), f), np.zeros((P, SCOLS), f)
    for b in range(Q4):
        for c in range(GROUP_CLIPS):
            mask_q[32 * b + c] = (slot % 32 < GT) & (slot % 32 // FRAMES == c)
            mask_k[32 * b + c] = np.where(np.arange(SCOLS) % GT // FRAMES == c, 0.0, -2.0 ** 100)
    small[:, COL_B1] = np.tile(a["L0_tok_b1"], PER)
    small[:, COL_B2] = np.tile(a["L0_tok_b2"], 2)
    small[:, COL_B3:COL_B3 + 2] = a["L0_tok_b3"].reshape(KC, P).T
    small[:, COL_B4:COL_B4 + 2] = a["L0_tok_b4"].reshape(KC, P).T
    small[:, COL_FREQ:COL_FREQ + 32] = np.tile(np.repeat(a["L0_tok_rope_freqs"], 2), 2)
    arrays["small"] = small
    w = np.zeros((3, PER, C1, 2, C2), f)
    for second in range(2):
        for j in range(K2):
            at = PER * (1 + second) - PAD2 + j
            w[at // PER, at % PER, :, second] = a["L0_tok_w2"][:, :, j].T
    arrays["w2"] = w.reshape(3, P, P).transpose(1, 0, 2)
    w = np.zeros((PARITIES, 2 * PAIRS, C2, C3), f)
    for odd in range(PARITIES):
        w[odd, odd:odd + K3] = a["L0_tok_w3"].transpose(2, 1, 0)
    arrays["w3"] = w.reshape(PARITIES, PAIRS, P, C3).transpose(2, 0, 1, 3)
    w = np.zeros((P, KC, 3, P), f)
    per_group = a["L0_tok_w4"].shape[1]
    for o in range(DIM):
        first = o % P // per_group * per_group
        w[first:first + per_group, o // P, :, o % P] = a["L0_tok_w4"][o]
    w5 = a["L0_tok_w5"][:, :, 0].T.reshape(KC, P, DIM).transpose(1, 0, 2)
    arrays["w45"] = np.concatenate([w.reshape(P, -1), w5.reshape(P, -1)], 1)
    arrays["rows"] = np.concatenate([a[k] for k in ("L0_tok_norm_w", "L0_attn_b_out", "L0_attn_ln_gamma",
                                                    "L0_attn_ln_beta", "L0_tok_b5")]).reshape(1, ROWS * DIM)
    gate = a["L0_ffn_Wg"].reshape(KC, P, EXPERTS).transpose(1, 0, 2).reshape(P, -1)
    arrays["consts"] = np.concatenate([np.eye(P, dtype=f), mask_q, mask_k, gate], 1)
    arrays["w_qkv"] = a["L0_attn_w_qkv"]
    arrays["w_out"] = a["L0_attn_w_out"]
    arrays["W1"] = a["L0_ffn_W1"]
    arrays["W2"] = a["L0_ffn_W2"]

    nc = bacc.Bacc("TRN2", target_bir_lowering=False, num_devices=1)
    sent, args = {}, []
    for name, value in arrays.items():
        sent[f"in_{name}"] = np.ascontiguousarray(value)
        args.append(nc.dram_tensor(f"in_{name}", value.shape, mybir.dt.from_np(value.dtype), kind="ExternalInput").ap())
    out = nc.dram_tensor("out_tokens", _OUT[0], mybir.dt.from_np(np.dtype(_OUT[1])), kind="ExternalOutput").ap()
    build(nc, *args, out)
    return run_bass_kernel_spmd(nc, [sent], core_ids=[0]).results[0]["out_tokens"]
```
